# Optimizing a Trainium2 kernel written in Bass

```python
import numpy as np
import jax
import jax.numpy as jnp

def _softmax(x, axis=-1):
    return jax.nn.softmax(x, axis=axis)
def _gelu(x):
    return jax.nn.gelu(x, approximate=True)
def _silu(x):
    return jax.nn.silu(x)
def _sigmoid(x):
    return jax.nn.sigmoid(x)
def _layernorm(x, axis=-1, eps=1e-5):
    m = jnp.mean(x, axis=axis, keepdims=True)
    v = jnp.var(x, axis=axis, keepdims=True)
    return (x - m) / jnp.sqrt(v + eps)
def _scatter_add(tgt, idx, src, axis=0):
    return tgt.at[idx].add(src)
def _segment_sum(src, seg, n):
    return jax.ops.segment_sum(src, seg, n)

kernel_name = 'mk_conv_seq_d2_conv_nchw96_66e280'

def setup_inputs(seed: int = 0):
    np.random.seed(seed)
    _w = jnp.asarray
    def _rec_inputs():
        import jax
        import jax.numpy as jnp
        _gk = jax.random.key(seed)
        x = 7.572e-06 + 1 * jax.random.normal(jax.random.fold_in(_gk, 1), (32, 96, 56, 56), jnp.float32)
        return x
    x = _rec_inputs()
    def _L0_conv_setup():
        import jax, jax.numpy as jnp
        import numpy as np
        EPS = 1e-05

        def _bn(x, gamma, beta, mean, var):
            inv = jax.lax.rsqrt(var + EPS)
            return (x - mean[None, :, None, None]) * (gamma * inv)[None, :, None, None] + beta[None, :, None, None]

        def _conv(x, w, stride=1, padding=0, groups=1):
            return jax.lax.conv_general_dilated(x, w, window_strides=(stride, stride), padding=[(padding, padding), (padding, padding)], dimension_numbers=('NCHW', 'OIHW', 'NCHW'), feature_group_count=groups)
        key = jax.random.key(seed)
        ks = jax.random.split(key, 8)
        C, E, Cout = (96, 6, 96)
        M = C * E
        x = jax.random.normal(ks[0], (32, C, 56, 56), dtype=jnp.float32)
        w1 = jax.random.normal(ks[1], (M, C, 1, 1), dtype=jnp.float32) * 0.05
        g1 = jnp.ones((M,), jnp.float32)
        b1 = jnp.zeros((M,), jnp.float32)
        m1 = jax.random.normal(ks[2], (M,), jnp.float32) * 0.1
        v1 = jax.random.uniform(ks[3], (M,), jnp.float32, 0.5, 1.5)
        wd = jax.random.normal(ks[4], (M, 1, 3, 3), dtype=jnp.float32) * 0.1
        g2 = jnp.ones((M,), jnp.float32)
        b2 = jnp.zeros((M,), jnp.float32)
        m2 = jax.random.normal(ks[5], (M,), jnp.float32) * 0.1
        v2 = jax.random.uniform(ks[6], (M,), jnp.float32, 0.5, 1.5)
        w3 = jax.random.normal(ks[7], (Cout, M, 1, 1), dtype=jnp.float32) * 0.05
        g3 = jnp.ones((Cout,), jnp.float32)
        b3 = jnp.zeros((Cout,), jnp.float32)
        m3 = jnp.zeros((Cout,), jnp.float32)
        v3 = jnp.ones((Cout,), jnp.float32)
        return {'x': x, 'w1': w1, 'g1': g1, 'b1': b1, 'm1': m1, 'v1': v1, 'wd': wd, 'g2': g2, 'b2': b2, 'm2': m2, 'v2': v2, 'w3': w3, 'g3': g3, 'b3': b3, 'm3': m3, 'v3': v3}
    _L0_conv_all = _L0_conv_setup()
    _L0_conv_in = {k: v for k, v in _L0_conv_all.items() if k in ('w1', 'g1', 'b1', 'm1', 'v1', 'wd', 'g2', 'b2', 'm2', 'v2', 'w3', 'g3', 'b3', 'm3', 'v3', )}
    del _L0_conv_all

    def _L1_conv_setup():
        import jax, jax.numpy as jnp
        import numpy as np
        B, C, H, W = (4, 96, 64, 64)
        CS = 8
        DN = 2 * C
        N = 16
        K = 4
        DT_R = (C + 15) // 16
        EPS = 1e-05

        def _ln(x, g, b):
            m = x.mean(-1, keepdims=True)
            v = ((x - m) ** 2).mean(-1, keepdims=True)
            return (x - m) / jnp.sqrt(v + EPS) * g + b

        def _selective_scan(xs, delta, A, Bs, Cs, D):
            Bc, Kk, Dn, L = xs.shape
            uT = xs.transpose(3, 0, 1, 2)
            dT = delta.transpose(3, 0, 1, 2)
            BT = Bs.transpose(3, 0, 1, 2)
            CT = Cs.transpose(3, 0, 1, 2)

            def step(h, inp):
                u_l, d_l, B_l, C_l = inp
                dA = jnp.exp(d_l[..., None] * A)
                h = h * dA + (d_l * u_l)[..., None] * B_l[:, :, None, :]
                y = jnp.einsum('bkdn,bkn->bkd', h, C_l)
                return (h, y)
            h0 = jnp.zeros((Bc, Kk, Dn, A.shape[-1]), xs.dtype)
            _, ys = jax.lax.scan(step, h0, (uT, dT, BT, CT))
            ys = ys.transpose(1, 2, 3, 0)
            return ys + D[None, :, :, None] * xs

        def _ss2d(xh, in_proj_w, conv_w, conv_b, x_proj_w, dt_w, dt_b, A_logs, Ds, outnorm_g, outnorm_b, out_proj_w):
            Bc, Hc, Wc, _ = xh.shape
            L = Hc * Wc
            xz = xh @ in_proj_w
            xc, z = jnp.split(xz, 2, axis=-1)
            xc = xc.transpose(0, 3, 1, 2)
            xc = jax.lax.conv_general_dilated(xc, conv_w, (1, 1), ((1, 1), (1, 1)), feature_group_count=DN)
            xc = jax.nn.silu(xc + conv_b[None, :, None, None])
            x0 = xc.reshape(Bc, DN, L)
            x1 = xc.transpose(0, 1, 3, 2).reshape(Bc, DN, L)
            xs = jnp.stack([x0, x1, x0[:, :, ::-1], x1[:, :, ::-1]], axis=1)
            x_dbl = jnp.einsum('bkdl,kcd->bkcl', xs, x_proj_w)
            dts = x_dbl[:, :, :DT_R]
            Bs = x_dbl[:, :, DT_R:DT_R + N]
            Cs = x_dbl[:, :, DT_R + N:]
            dts = jnp.einsum('bkrl,kdr->bkdl', dts, dt_w)
            delta = jax.nn.softplus(dts + dt_b[None, :, :, None])
            A = -jnp.exp(A_logs).reshape(K, DN, N)
            ys = _selective_scan(xs, delta, A, Bs, Cs, Ds.reshape(K, DN))
            y0 = ys[:, 0]
            y1 = ys[:, 1].reshape(Bc, DN, Wc, Hc).transpose(0, 1, 3, 2).reshape(Bc, DN, L)
            y2 = ys[:, 2, :, ::-1]
            y3 = ys[:, 3, :, ::-1].reshape(Bc, DN, Wc, Hc).transpose(0, 1, 3, 2).reshape(Bc, DN, L)
            y = (y0 + y1 + y2 + y3).transpose(0, 2, 1)
            y = _ln(y, outnorm_g, outnorm_b).reshape(Bc, Hc, Wc, DN)
            y = y * jax.nn.silu(z)
            return y @ out_proj_w
        key = jax.random.key(seed)
        ks = jax.random.split(key, 12)
        s = 0.02
        inp = {'x': jax.random.normal(ks[0], (B, C, H, W), jnp.float32), 'gamma': jnp.ones((C,), jnp.float32), 'beta': jnp.zeros((C,), jnp.float32), 'alpha': jnp.float32(0.5), 'ln1_g': jnp.ones((C,), jnp.float32), 'ln1_b': jnp.zeros((C,), jnp.float32), 'in_proj_w': jax.random.normal(ks[1], (C, 2 * DN), jnp.float32) / np.sqrt(C), 'conv_w': jax.random.normal(ks[2], (DN, 1, 3, 3), jnp.float32) / 3.0, 'conv_b': jnp.zeros((DN,), jnp.float32), 'x_proj_w': jax.random.normal(ks[3], (K, DT_R + 2 * N, DN), jnp.float32) / np.sqrt(DN), 'dt_w': jax.random.normal(ks[4], (K, DN, DT_R), jnp.float32) * DT_R ** (-0.5), 'dt_b': jnp.full((K, DN), -4.6, jnp.float32) + s * jax.random.normal(ks[5], (K, DN), jnp.float32), 'A_logs': jnp.log(jnp.broadcast_to(jnp.arange(1, N + 1, dtype=jnp.float32), (K * DN, N))).copy(), 'Ds': jnp.ones((K * DN,), jnp.float32), 'outnorm_g': jnp.ones((DN,), jnp.float32), 'outnorm_b': jnp.zeros((DN,), jnp.float32), 'out_proj_w': jax.random.normal(ks[6], (DN, C), jnp.float32) / np.sqrt(DN)}
        return inp
    _L1_conv_all = _L1_conv_setup()
    _L1_conv_in = {k: v for k, v in _L1_conv_all.items() if k in ('gamma', 'beta', 'alpha', 'ln1_g', 'ln1_b', 'in_proj_w', 'conv_w', 'conv_b', 'x_proj_w', 'dt_w', 'dt_b', 'A_logs', 'Ds', 'outnorm_g', 'outnorm_b', 'out_proj_w', )}
    del _L1_conv_all

    return {
        "x": x,
        "L0_conv_w1": _L0_conv_in["w1"],
        "L0_conv_g1": _L0_conv_in["g1"],
        "L0_conv_b1": _L0_conv_in["b1"],
        "L0_conv_m1": _L0_conv_in["m1"],
        "L0_conv_v1": _L0_conv_in["v1"],
        "L0_conv_wd": _L0_conv_in["wd"],
        "L0_conv_g2": _L0_conv_in["g2"],
        "L0_conv_b2": _L0_conv_in["b2"],
        "L0_conv_m2": _L0_conv_in["m2"],
        "L0_conv_v2": _L0_conv_in["v2"],
        "L0_conv_w3": _L0_conv_in["w3"],
        "L0_conv_g3": _L0_conv_in["g3"],
        "L0_conv_b3": _L0_conv_in["b3"],
        "L0_conv_m3": _L0_conv_in["m3"],
        "L0_conv_v3": _L0_conv_in["v3"],
        "L1_conv_gamma": _L1_conv_in["gamma"],
        "L1_conv_beta": _L1_conv_in["beta"],
        "L1_conv_alpha": _L1_conv_in["alpha"],
        "L1_conv_ln1_g": _L1_conv_in["ln1_g"],
        "L1_conv_ln1_b": _L1_conv_in["ln1_b"],
        "L1_conv_in_proj_w": _L1_conv_in["in_proj_w"],
        "L1_conv_conv_w": _L1_conv_in["conv_w"],
        "L1_conv_conv_b": _L1_conv_in["conv_b"],
        "L1_conv_x_proj_w": _L1_conv_in["x_proj_w"],
        "L1_conv_dt_w": _L1_conv_in["dt_w"],
        "L1_conv_dt_b": _L1_conv_in["dt_b"],
        "L1_conv_A_logs": _L1_conv_in["A_logs"],
        "L1_conv_Ds": _L1_conv_in["Ds"],
        "L1_conv_outnorm_g": _L1_conv_in["outnorm_g"],
        "L1_conv_outnorm_b": _L1_conv_in["outnorm_b"],
        "L1_conv_out_proj_w": _L1_conv_in["out_proj_w"],
    }

def reference(x, L0_conv_w1, L0_conv_g1, L0_conv_b1, L0_conv_m1, L0_conv_v1, L0_conv_wd, L0_conv_g2, L0_conv_b2, L0_conv_m2, L0_conv_v2, L0_conv_w3, L0_conv_g3, L0_conv_b3, L0_conv_m3, L0_conv_v3, L1_conv_gamma, L1_conv_beta, L1_conv_alpha, L1_conv_ln1_g, L1_conv_ln1_b, L1_conv_in_proj_w, L1_conv_conv_w, L1_conv_conv_b, L1_conv_x_proj_w, L1_conv_dt_w, L1_conv_dt_b, L1_conv_A_logs, L1_conv_Ds, L1_conv_outnorm_g, L1_conv_outnorm_b, L1_conv_out_proj_w):
    import jax
    import jax.numpy as jnp
    def _L0_conv_ref(x, w1, g1, b1, m1, v1, wd, g2, b2, m2, v2, w3, g3, b3, m3, v3):
        import jax, jax.numpy as jnp
        import numpy as np
        EPS = 1e-05

        def _bn(x, gamma, beta, mean, var):
            inv = jax.lax.rsqrt(var + EPS)
            return (x - mean[None, :, None, None]) * (gamma * inv)[None, :, None, None] + beta[None, :, None, None]

        def _conv(x, w, stride=1, padding=0, groups=1):
            return jax.lax.conv_general_dilated(x, w, window_strides=(stride, stride), padding=[(padding, padding), (padding, padding)], dimension_numbers=('NCHW', 'OIHW', 'NCHW'), feature_group_count=groups)
        M = wd.shape[0]
        out = jax.nn.relu(_bn(_conv(x, w1), g1, b1, m1, v1))
        out = jax.nn.relu(_bn(_conv(out, wd, stride=1, padding=1, groups=M), g2, b2, m2, v2))
        out = _bn(_conv(out, w3), g3, b3, m3, v3)
        return out + x

    def _L1_conv_ref(x, gamma, beta, alpha, ln1_g, ln1_b, in_proj_w, conv_w, conv_b, x_proj_w, dt_w, dt_b, A_logs, Ds, outnorm_g, outnorm_b, out_proj_w):
        import jax, jax.numpy as jnp
        import numpy as np
        B, C, H, W = (4, 96, 64, 64)
        CS = 8
        DN = 2 * C
        N = 16
        K = 4
        DT_R = (C + 15) // 16
        EPS = 1e-05

        def _ln(x, g, b):
            m = x.mean(-1, keepdims=True)
            v = ((x - m) ** 2).mean(-1, keepdims=True)
            return (x - m) / jnp.sqrt(v + EPS) * g + b

        def _selective_scan(xs, delta, A, Bs, Cs, D):
            Bc, Kk, Dn, L = xs.shape
            uT = xs.transpose(3, 0, 1, 2)
            dT = delta.transpose(3, 0, 1, 2)
            BT = Bs.transpose(3, 0, 1, 2)
            CT = Cs.transpose(3, 0, 1, 2)

            def step(h, inp):
                u_l, d_l, B_l, C_l = inp
                dA = jnp.exp(d_l[..., None] * A)
                h = h * dA + (d_l * u_l)[..., None] * B_l[:, :, None, :]
                y = jnp.einsum('bkdn,bkn->bkd', h, C_l)
                return (h, y)
            h0 = jnp.zeros((Bc, Kk, Dn, A.shape[-1]), xs.dtype)
            _, ys = jax.lax.scan(step, h0, (uT, dT, BT, CT))
            ys = ys.transpose(1, 2, 3, 0)
            return ys + D[None, :, :, None] * xs

        def _ss2d(xh, in_proj_w, conv_w, conv_b, x_proj_w, dt_w, dt_b, A_logs, Ds, outnorm_g, outnorm_b, out_proj_w):
            Bc, Hc, Wc, _ = xh.shape
            L = Hc * Wc
            xz = xh @ in_proj_w
            xc, z = jnp.split(xz, 2, axis=-1)
            xc = xc.transpose(0, 3, 1, 2)
            xc = jax.lax.conv_general_dilated(xc, conv_w, (1, 1), ((1, 1), (1, 1)), feature_group_count=DN)
            xc = jax.nn.silu(xc + conv_b[None, :, None, None])
            x0 = xc.reshape(Bc, DN, L)
            x1 = xc.transpose(0, 1, 3, 2).reshape(Bc, DN, L)
            xs = jnp.stack([x0, x1, x0[:, :, ::-1], x1[:, :, ::-1]], axis=1)
            x_dbl = jnp.einsum('bkdl,kcd->bkcl', xs, x_proj_w)
            dts = x_dbl[:, :, :DT_R]
            Bs = x_dbl[:, :, DT_R:DT_R + N]
            Cs = x_dbl[:, :, DT_R + N:]
            dts = jnp.einsum('bkrl,kdr->bkdl', dts, dt_w)
            delta = jax.nn.softplus(dts + dt_b[None, :, :, None])
            A = -jnp.exp(A_logs).reshape(K, DN, N)
            ys = _selective_scan(xs, delta, A, Bs, Cs, Ds.reshape(K, DN))
            y0 = ys[:, 0]
            y1 = ys[:, 1].reshape(Bc, DN, Wc, Hc).transpose(0, 1, 3, 2).reshape(Bc, DN, L)
            y2 = ys[:, 2, :, ::-1]
            y3 = ys[:, 3, :, ::-1].reshape(Bc, DN, Wc, Hc).transpose(0, 1, 3, 2).reshape(Bc, DN, L)
            y = (y0 + y1 + y2 + y3).transpose(0, 2, 1)
            y = _ln(y, outnorm_g, outnorm_b).reshape(Bc, Hc, Wc, DN)
            y = y * jax.nn.silu(z)
            return y @ out_proj_w
        Bb, Cc, Hh, Ww = x.shape
        mean = x.mean(axis=(2, 3), keepdims=True)
        var = ((x - mean) ** 2).mean(axis=(2, 3), keepdims=True)
        x_norm = (x - mean) / jnp.sqrt(var + EPS)
        x_norm = gamma[None, :, None, None] * x_norm + beta[None, :, None, None]
        x_act = jax.nn.silu(x_norm)
        hn, wn = (Hh // CS, Ww // CS)
        xc = x_act.reshape(Bb, Cc, hn, CS, wn, CS).transpose(0, 2, 4, 1, 3, 5)
        xc = xc.reshape(Bb * hn * wn, Cc, CS, CS)
        h = xc.transpose(0, 2, 3, 1)
        h = h + _ss2d(_ln(h, ln1_g, ln1_b), in_proj_w, conv_w, conv_b, x_proj_w, dt_w, dt_b, A_logs, Ds, outnorm_g, outnorm_b, out_proj_w)
        xv = h.transpose(0, 3, 1, 2)
        xv = xv.reshape(Bb, hn, wn, Cc, CS, CS).transpose(0, 3, 1, 4, 2, 5)
        xv = xv.reshape(Bb, Cc, Hh, Ww)
        return x + alpha * xv

    def _gn(v, G=32, eps=1e-5):
        B_, C_, H_, W_ = v.shape
        g = v.reshape(B_, G, C_ // G, H_, W_)
        m = jnp.mean(g, axis=(2, 3, 4), keepdims=True)
        s = jnp.var(g, axis=(2, 3, 4), keepdims=True)
        return ((g - m) / jnp.sqrt(s + eps)).reshape(v.shape)

    def _ln_c(v, eps=1e-6):
        m = jnp.mean(v, axis=1, keepdims=True)
        s = jnp.var(v, axis=1, keepdims=True)
        return (v - m) / jnp.sqrt(s + eps)

    def _ln_t(v, eps=1e-5):
        m = jnp.mean(v, axis=-1, keepdims=True)
        s = jnp.var(v, axis=-1, keepdims=True)
        return (v - m) / jnp.sqrt(s + eps)

    def _to_tokens(v):
        B_, C_, H_, W_ = v.shape
        return v.reshape(B_, C_, H_ * W_).transpose(0, 2, 1)
    def _from_tokens(t, like):
        B_, C_, H_, W_ = like.shape
        return t.transpose(0, 2, 1).reshape(B_, C_, H_, W_)

    x = _L0_conv_ref(x, L0_conv_w1, L0_conv_g1, L0_conv_b1, L0_conv_m1, L0_conv_v1, L0_conv_wd, L0_conv_g2, L0_conv_b2, L0_conv_m2, L0_conv_v2, L0_conv_w3, L0_conv_g3, L0_conv_b3, L0_conv_m3, L0_conv_v3)
    x = _L1_conv_ref(x, L1_conv_gamma, L1_conv_beta, L1_conv_alpha, L1_conv_ln1_g, L1_conv_ln1_b, L1_conv_in_proj_w, L1_conv_conv_w, L1_conv_conv_b, L1_conv_x_proj_w, L1_conv_dt_w, L1_conv_dt_b, L1_conv_A_logs, L1_conv_Ds, L1_conv_outnorm_g, L1_conv_outnorm_b, L1_conv_out_proj_w)
    return x


_drawn_inputs = setup_inputs


def setup_inputs(seed=0):
    import zlib

    import numpy as np

    out = dict(_drawn_inputs(seed))
    spreads = {'L0_conv_g1': (1.0, 0.6),
     'L0_conv_b1': (0.0, 0.439),
     'L0_conv_g2': (1.0, 0.6),
     'L0_conv_b2': (0.0, 0.1),
     'L0_conv_g3': (1.0, 0.6),
     'L0_conv_b3': (0.0, 0.1),
     'L0_conv_m3': (0.0, 0.1),
     'L0_conv_v3': (1.0, 0.6),
     'L1_conv_gamma': (1.0, 0.2),
     'L1_conv_beta': (0.0, 0.1),
     'L1_conv_ln1_g': (1.0, 0.2),
     'L1_conv_ln1_b': (0.0, 0.1),
     'L1_conv_conv_b': (0.0, 0.308),
     'L1_conv_Ds': (1.0, 0.6),
     'L1_conv_outnorm_g': (1.0, 0.2),
     'L1_conv_outnorm_b': (0.0, 0.331)}
    factors = {'L0_conv_m1': 2.834,
     'L0_conv_v1': 3.322,
     'L0_conv_v2': 2.776,
     'L1_conv_x_proj_w': 7.869,
     'L1_conv_dt_w': 8.0,
     'L1_conv_dt_b': 8.0,
     'L1_conv_A_logs': 8.0}
    for name, (base, spread) in spreads.items():
        noise = np.random.default_rng([zlib.crc32(name.encode()), seed]).standard_normal(out[name].shape)
        drawn = base * np.exp(spread * noise) if base else spread * noise
        out[name] = jnp.asarray(drawn.astype(out[name].dtype))
    for name, factor in factors.items():
        out[name] = (out[name] * factor).astype(out[name].dtype)
    return out
```

```python
import concourse.bass as bass
from concourse import mybir
from contextlib import ExitStack
import numpy as np

B, C, HW, WS = 32, 96, 56, 8
NWR = HW // WS
NP = WS * HW
WP = WS * WS
HALO = (WS + 2) * HW
HH = HALO // 2
CHUNKS = B * NWR
E6, MT = 6 * C, 5
DN, NS, K, DTR = 2 * C, 16, 4, C // 16
DB = DN - 128
TILES = 6
PAIRS = 8
SLOTS = TILES * PAIRS
XP = WS + 2
EPS = 1e-5
LN_SMALL = 2.0 ** -11
EXP_CAP = 2.0 ** 60


def rows_of(t):
    return min(128, E6 - 128 * t)


PACK = [("w1", E6), ("w3", MT * C), ("wd", MT * 9),
        ("g1", MT), ("b1", MT), ("m1", MT), ("v1", MT), ("g2", MT), ("b2", MT), ("m2", MT), ("v2", MT),
        ("g3", 1), ("b3", 1), ("m3", 1), ("v3", 1),
        ("gamma", 1), ("beta", 1), ("alpha", 1), ("lng", 1), ("lnb", 1), ("inw", 512),
        ("cwa", 9), ("cwb", 9), ("cba", 1), ("cbb", 1),
        ("xpa", K * 128), ("xpb", 2 * 128), ("dta", K * 128), ("dtm", K * DB), ("dtb", TILES),
        ("alog", TILES * NS), ("dsa", K), ("dsm", K), ("oga", 1), ("oba", 1), ("ogb", 1), ("obb", 1),
        ("owa", C), ("owb", C),
        ("cen96", C), ("one96", C), ("cenaa", 128), ("cenalo", 128), ("cenahi", 128),
        ("cenba", DB), ("cenblo", DB), ("cenbhi", DB), ("one192", 128), ("ident", 128), ("selcol", 32)]
COL, _at = {}, 0
for _name, _n in PACK:
    COL[_name] = (_at, _n)
    _at += _n
PACKED = _at

SIDE = [("xp2", 1, 3), ("xp3", 1, 3), ("up0_0", 3, 4), ("up0_1", 4, 5), ("cenA", 5, 6), ("cenB", 5, 6),
        ("dt3", 6, 7), ("center", 7, 8), ("varY", 7, 8), ("dt4", 9, 10), ("var", 9, 10),
        ("up1_0", 10, 11), ("up1_1", 11, 12), ("dt5", 12, 13), ("outp", 12, 13),
        ("inA", 13, 14), ("inB", 13, 14), ("inZA", 14, 15), ("inZB", 14, 15), ("convA", 15, 16),
        ("convB", 17, 18), ("up2_0", 17, 18), ("up2_1", 18, 19), ("up3_0", 24, 25), ("up3_1", 25, 26),
        ("xp0", 28, 30), ("xp1", 28, 30), ("up4_0", 31, 32), ("dt0", 31, 32), ("up4_1", 32, 33),
        ("dt1", 34, 35), ("dt2", 37, 38), ("down", 44, 45)]
assert all(SIDE[i][1] >= SIDE[i - 2][2] for i in range(2, len(SIDE)))
L0_SIDE = [f"up{t}_{h}" for t in range(MT) for h in range(2)] + ["down"]
F_SIDE = ["cenA", "cenB", "varY", "outp"]
DT_SLOT = {int(name[2:]): slot for name, slot, _ in SIDE if name.startswith("dt")}
DT_TURN = {t: i for i, t in enumerate([3, 4, 5, 0, 1, 2])}


class SideBanks:

    def __init__(self, names, before):
        self.at = {x: (i % 2, i // 2) for i, x in enumerate(names)}
        self.per = [(len(names) + 1) // 2, len(names) // 2]
        self.before = before

    def bank(self, name):
        return self.at[name][0]

    def fills(self, name, n):
        bank, nth = self.at[name]
        return self.before[bank] + nth + 1 + self.per[bank] * n

    def after(self, n):
        return [self.before[i] + self.per[i] * n for i in range(2)]


def build(nc, x_dev, pack, mask, x1_dram, out):
    fp32, bf16 = mybir.dt.float32, mybir.dt.bfloat16
    ALU, ACT = mybir.AluOpType, mybir.ActivationFunctionType
    ctx = ExitStack()
    with ctx:
        def sb(name, shape, dt=fp32):
            return ctx.enter_context(nc.sbuf_tensor(name, shape, dt))

        def sem(name):
            return ctx.enter_context(nc.semaphore(name))

        W = sb("weights", [128, PACKED])

        def w(name, rows=128, a=0, n=None):
            at, width = COL[name]
            return W[0:rows, at + a:at + (width if n is None else a + n)]

        words = [("mid", MT * XP * (HW + 2)), ("xpA", NWR * XP * XP), ("xpB", NWR * XP * XP),
                 ("dA", 2 * (2 * NP + 1)), ("h", 3 * 2 * NP), ("hC", 2 * 2 * NP), ("Q", K * NP // 2), ("uA", NP), ("uAT", NP), ("uM", NP),
                 ("delta", TILES * NP), ("dtu", TILES * NP), ("ysA", NP), ("ysAT", NP), ("ysM", NP),
                 ("gateP", 2 * NP), ("gateF", 2 * NP), ("residP", NP), ("residF", NP)]
        Z = sb("zeroed_once", [128, sum(n for _, n in words)])
        len_a = sum(n for _, n in words) * 2 // 3
        sb_eps = sb("eps", [128, 1])
        z, at = {}, 0
        for name, n in words:
            z[name] = Z[:, at:at + n]
            at += n
        mid = z["mid"].rearrange("p (t r c) -> p t r c", t=MT, r=XP)
        xpA = z["xpA"].rearrange("p (w i j) -> p w i j", w=NWR, i=XP)
        xpB = z["xpB"].rearrange("p (w i j) -> p w i j", w=NWR, i=XP)
        dA = z["dA"].rearrange("p (s f) -> p s f", s=2)
        h = z["h"].rearrange("p (s f) -> p s f", s=3)
        hC = z["hC"].rearrange("p (s f) -> p s f", s=2)
        Q = z["Q"].bitcast(bf16).rearrange("p (k f) -> p k f", k=K)
        uA, uAT, uM = z["uA"], z["uAT"], z["uM"]
        delta = z["delta"].rearrange("p (t f) -> p t f", t=TILES)
        dtu = z["dtu"].rearrange("p (t f) -> p t f", t=TILES)
        ysA, ysAT, ysM = z["ysA"], z["ysAT"], z["ysM"]
        gateP = z["gateP"].rearrange("p (a f) -> p a f", a=2)
        gateF = z["gateF"].rearrange("p (a f) -> p a f", a=2)
        residP, residF = z["residP"], z["residF"]

        sel = sb("sel", [128, 32, 128], bf16)
        diagA = sb("diagA", [128, 9, 128])
        diagB = sb("diagB", [128, 9, 128])
        masks = sb("masks", [128, NWR * 2 * HW])
        A = sb("A", [128, TILES * NS])
        s1, o1 = sb("s1", [128, MT]), sb("o1", [128, MT])
        s2, o2 = sb("s2", [128, MT]), sb("o2", [128, MT])
        s3, o3 = sb("s3", [128, 1]), sb("o3", [128, 1])
        inbias = sb("inbias", [128, 4])
        Dm = sb("Dm", [128, 2])
        xin = sb("xin", [C, HALO])
        acc = sb("acc", [128, 2, NP])
        z2 = sb("z2", [128, MT, NP])
        y3 = sb("y3", [C, NP])
        x1o = sb("x1o", [C, NP])
        stats = sb("stats", [C, NWR * 6])
        meanvar = sb("meanvar", [C, 2])
        coef = sb("coef", [C, 4])
        x1r = sb("x1r", [C, NP])
        v = sb("v", [C, NP])
        sigh = sb("sigh", [C, NP])
        h0 = sb("h0", [C, NP])
        cen = sb("cen", [C, NP])
        sq = sb("sq", [C, NP])
        vz = sb("vz", [128, 2, NP])
        sigz = sb("sigz", [128, 2, NP])
        vu = sb("vu", [128, 2, NP])
        sigu = sb("sigu", [128, 2, NP])
        Fk = sb("Fk", [64, 2, NP])
        rest = sb("rest", [128, 2, NP])
        dta_, dtm_ = sb("dt_abs", [128, 2, NP]), sb("dt_pos", [128, 2, NP])
        dte, dtl = sb("dt_exp", [128, 2, NP]), dta_
        dtp = sb("dt_poly", [128, 2, NP])
        Bsb = sb("Bsb", [128, 2, 2 * NP])
        dBu = sb("dBu", [128, 2, 2 * NP])
        yAs, rY = sigz[:, 0, :], sigz[:, 1, :]
        cY, sY = vu, sigu
        outs = sb("outs", [C, NP])
        outb = sb("outb", [C, NP])

        psum = ctx.enter_context(nc.psum_tensor("psum", [128, 8, 512], fp32))
        psB, psC, psY, side = psum[:, 0:2, :], psum[:, 2:4, :], psum[:, 4:6, :], psum[:, 6:8, :]

        def win(ap):
            return ap.rearrange("p (w i j) -> p w i j", i=WS, j=WS)

        def turned(ap):
            return ap.rearrange("p (w i j) -> p w j i", i=WS, j=WS)

        def image_rows(ap):
            return ap.rearrange("p (i w j) -> p w i j", i=WS, j=WS)

        names = """packed zeroed_a zeroed_b folded_bn folded_ready ident_ready dsum inw_done seeded bn_ln bn_rs inb
            x_loaded mid_masked taps z2_made x1_made x1_stored stats_made aggregated rstd_ln rstd_made scale_made coef_made
            x1_loaded v_made eh_made e1h_made lh_made sgh_made h0_made lnx_made rs_made xn_made
            vz_made ez_made e1z_made lz_made sgz_made gate_made vu_made eu_made e1u_made lu_made sgu_made
            alphah_made resid_made u_made ut_made um_made
            f_made q_mid q_lo abs_made exp_made log_made poly0_made poly_made
            logsel_made logmax_made delta_made dtu_made
            b_bcast b_evac c_bcast da_made dbu_made scanned cmult reduced y_evac
            yas_made sy_made lny_made ry_made norm_made gated outs_made out_made out_stored rotated masks_in""".split()
        S = {x: sem(x) for x in names}
        side_ready = [sem("side_ready0"), sem("side_ready1")]
        side_read = [sem("side_read0"), sem("side_read1")]
        passed = {e: sem(f"passed_{i}") for i, e in enumerate((nc.tensor.engine, nc.vector.engine, nc.gpsimd.engine))}
        CREDIT = {"z2_made": 1, "scanned": 2, "dbu_made": 2, "cmult": 1, "delta_made": 2, "dtu_made": 2}

        sides_l0 = SideBanks(L0_SIDE, [0, 0])
        sides = SideBanks([x for x, _, _ in SIDE], sides_l0.after(NWR))
        sides_f = SideBanks(F_SIDE, sides.after(CHUNKS + 1))

        def wait_side(eng, ph, name, n):
            eng.wait_ge(side_ready[ph.bank(name)], ph.fills(name, n))

        def wait_read(eng, ph, name, n):
            eng.wait_ge(side_read[ph.bank(name)], ph.fills(name, n))

        def wait_apart(eng, semaphore, value):
            eng.wait_ge(semaphore, value)
            eng.sem_inc(passed[eng.engine], 1)

        def side_ps(ph, name, width=NP, rows=128):
            return side[0:rows, ph.bank(name), 0:width]

        def over_chunks(eng, l0_only, boundary, iteration, last):
            with eng.Fori(0, NWR) as r:
                l0_only(r, r)
            boundary(0)
            with eng.Fori(0, B) as b:
                with eng.Fori(0, NWR) as r:
                    n = eng.snap(b * NWR + r)
                    iteration(n, b, r)
                boundary(b + 1)
            iteration(CHUNKS, B, 0)
            last(CHUNKS + 1)

        block = ctx.enter_context(nc.Block())

        @block.sync
        def _(sp):
            sp.dma_start(W[:, :], pack).then_inc(S["packed"], 16)
            sp.dma_start(masks[:, :], mask).then_inc(S["masks_in"], 16)

            def load_x(m):
                sp.wait_ge(S["x1_made"], m)
                sp.dma_start(xin[:, :], x_dev[bass.ds(m, 1)].rearrange("a c f -> (a c) f")).then_inc(S["x_loaded"], 16)

            def store_x1(m):
                sp.wait_ge(S["x1_made"], m + 1)
                sp.dma_start(x1_dram[bass.ds(m, 1)].rearrange("a c f -> (a c) f"), x1o[:, :]).then_inc(S["x1_stored"], 16)

            def store_out(f):
                sp.wait_ge(S["out_made"], f + 1)
                sp.dma_start(out[bass.ds(f, 1)].rearrange("a c f -> (a c) f"), outb[:, :]).then_inc(S["out_stored"], 16)

            def l0_only(m, r):
                load_x(m)
                store_x1(m)

            def iteration(n, b, r):
                load_x(n + NWR)
                sp.wait_ge(S["x1_stored"], 16 * n + 16)
                sp.wait_ge(S["resid_made"], n)
                sp.dma_start(x1r[:, :], x1_dram[bass.ds(n, 1)].rearrange("a c f -> (a c) f")).then_inc(S["x1_loaded"], 16)
                store_out(n)
                sp.wait_ge(S["gated"], n + 1)
                sp.wait_ge(S["gate_made"], n)
                sp.dma_start(gateF[:, :, :], gateP[:, :, :]).then_inc(S["rotated"], 16)
                sp.dma_start(residF[0:C, :], residP[0:C, :]).then_inc(S["rotated"], 16)
                store_x1(n + NWR)

            def last(f):
                store_out(f)

            sp.wait_ge(S["packed"], 16)
            over_chunks(sp, l0_only, lambda b: None, iteration, last)
            sp.wait_ge(S["x1_stored"], 16 * (CHUNKS + 1 + NWR))
            sp.wait_ge(S["out_stored"], 16 * (CHUNKS + 2))

        @block.tensor
        def _(pe):
            mm = nc.tensor.matmul
            order = []

            def open_side(ph, name, n):
                pe.wait_ge(side_read[ph.bank(name)], ph.fills(name, n) - 1)

            def done_side(ph, name, ins):
                order.append(name)
                ins.then_inc(side_ready[ph.bank(name)], 1)

            def up(ph, m, n, t, half):
                if t == 0 and half == 0:
                    pe.wait_ge(S["x_loaded"], 16 * m + 16)
                name = f"up{t}_{half}"
                open_side(ph, name, n)
                done_side(ph, name, mm(side_ps(ph, name, HH, rows_of(t)), w("w1", C, 128 * t, rows_of(t)),
                                       xin[:, HH * half:HH * half + HH], start=True, stop=True))

            def down(ph, m, n):
                pe.wait_ge(S["z2_made"], 5 * m + 5 + CREDIT["z2_made"])
                open_side(ph, "down", n)
                for t in range(MT):
                    ins = mm(side_ps(ph, "down", NP, C), w("w3", rows_of(t), C * t, C), z2[0:rows_of(t), t, :],
                             start=t == 0, stop=t == MT - 1)
                done_side(ph, "down", ins)

            def project_x(n, k):
                name = f"xp{k}"
                if k == 0:
                    pe.wait_ge(S["u_made"], n + 1)
                if k == 1:
                    pe.wait_ge(S["ut_made"], n + 1)
                    pe.wait_ge(S["um_made"], n + 1)
                open_side(sides, name, n)
                lo, src = (0, uA) if k % 2 == 0 else (DB, uAT)
                mm(side_ps(sides, name), w("xpa", 128, 128 * k, 128), src, start=True, stop=False)
                at = COL["xpb"][0] + 128 * (k // 2)
                done_side(sides, name, mm(side_ps(sides, name), W[lo:lo + DB, at:at + 128], uM[lo:lo + DB, :],
                                          start=False, stop=True))

            def steps(n, t):
                name = f"dt{t}"
                if t in (0, 3):
                    pe.wait_ge(S["f_made"], 4 * n + (2 if t == 3 else 4))
                if t % 3 < 2:
                    open_side(sides, name, n)
                else:
                    wait_apart(pe, side_read[sides.bank(name)], sides.fills(name, n) - 1)
                k0 = 0 if t < 3 else 2
                if t % 3 < 2:
                    k = k0 + t % 3
                    ins = mm(side_ps(sides, name), w("dta", 64, 128 * k, 128), Fk[:, k % 2, :], start=True, stop=True)
                else:
                    ps = side[:, sides.bank(name), 0:NP]
                    mm(ps[0:DB], w("dtm", 64, DB * k0, DB), Fk[:, 0, :], start=True, stop=True)
                    ins = mm(ps[DB:128], w("dtm", 64, DB * (k0 + 1), DB), Fk[:, 1, :], start=True, stop=True)
                done_side(sides, name, ins)

            def one(ph, name, n, lhs, rhs, rows):
                open_side(ph, name, n)
                done_side(ph, name, mm(side_ps(ph, name, NP, rows), lhs, rhs, start=True, stop=True))

            def in_project(n, j):
                name = ("inA", "inB", "inZA", "inZB")[j]
                one(sides, name, n, w("inw", C, 128 * j, 128), sq[:, :], 128)

            def window_conv(n, name, diag, xp):
                open_side(sides, name, n)
                for tap in range(9):
                    di, dj = tap // 3, tap % 3
                    ins = mm(side_ps(sides, name), diag[:, tap, :], xp[:, :, di:di + WS, dj:dj + WS],
                             start=tap == 0, stop=tap == 8)
                done_side(sides, name, ins)

            def broadcast(p, first_row, ps, done):
                t, n0 = p // PAIRS, 2 * (p % PAIRS)
                k0 = 0 if t < 3 else 2
                for j in range(2):
                    row = first_row + n0 + j
                    if t % 3 < 2:
                        ins = mm(ps[:, j, 0:NP], sel[:, row, :], Q[:, k0 + t % 3, :], start=True, stop=True)
                    else:
                        mm(ps[0:DB, j, 0:NP], sel[:, row, 0:DB], Q[:, k0, :], start=True, stop=True)
                        ins = mm(ps[DB:128, j, 0:NP], sel[:, row, 0:DB], Q[:, k0 + 1, :], start=True, stop=True)
                ins.then_inc(done, 1)

            def scan_slot(n, p):
                s = SLOTS * n + p
                if p < SLOTS:
                    if p == 0:
                        pe.wait_ge(S["q_lo"], 4 * n)
                    if p == 24:
                        pe.wait_ge(S["q_lo"], 4 * n + 2)
                    pe.wait_ge(S["b_evac"], s)
                    broadcast(p, 0, psB, S["b_bcast"])
                c_and_sum(n, p)

            def c_and_sum(n, p):
                s = SLOTS * n + p
                pe.wait_ge(S["cmult"], s - 1 + CREDIT["cmult"])
                broadcast((p - 2) % SLOTS, NS, psC, S["c_bcast"])
                q = (p - 3) % SLOTS
                t = q // PAIRS
                if q % PAIRS == 0:
                    pe.wait_ge(S["y_evac"], 6 * n + t)
                for j in range(2):
                    ins = mm(psY[:, t % 2, 0:NP], w("ident"), hC[:, q % 2, NP * j:NP * j + NP],
                             start=q % PAIRS == 0 and j == 0, stop=q % PAIRS == PAIRS - 1 and j == 1)
                ins.then_inc(S["reduced"], 1)

            def center_y(ph, f, n, name, wa, wlo, whi, rows):
                if name == "cenA":
                    pe.wait_ge(S["yas_made"], f + 1)
                    pe.wait_ge(S["y_evac"], 6 * f + 1)
                open_side(ph, name, n)
                ps = side_ps(ph, name, NP, rows)
                mm(ps, wa, yAs, start=True, stop=False)
                mm(ps, wlo, ysM, start=False, stop=False)
                done_side(ph, name, mm(ps, whi, turned(ysM), start=False, stop=True))

            def var_y(ph, n):
                wait_read(pe, ph, "cenA", n)
                wait_read(pe, ph, "cenB", n)
                open_side(ph, "varY", n)
                mm(side_ps(ph, "varY"), w("one192"), sY[:, 0, :], start=True, stop=False)
                done_side(ph, "varY", mm(side_ps(ph, "varY"), w("one192", DB), sY[0:DB, 1, :], start=False, stop=True))

            def out_project(ph, f, n):
                pe.wait_ge(S["gated"], f + 1)
                open_side(ph, "outp", n)
                mm(side_ps(ph, "outp", NP, C), w("owa"), cY[:, 0, :], start=True, stop=False)
                done_side(ph, "outp", mm(side_ps(ph, "outp", NP, C), w("owb", DB), cY[0:DB, 1, :], start=False, stop=True))

            def finish(ph, f, n, p):
                if p == 5:
                    center_y(ph, f, n, "cenA", w("cenaa"), w("cenalo"), w("cenahi"), 128)
                    center_y(ph, f, n, "cenB", w("cenba"), w("cenblo"), w("cenbhi"), DB)
                if p == 7:
                    var_y(ph, n)
                if p == 12:
                    out_project(ph, f, n)

            def l0_only(m, r):
                for t in range(MT):
                    up(sides_l0, m, m, t, 0)
                    up(sides_l0, m, m, t, 1)
                down(sides_l0, m, m)

            def iteration(n, b, r):
                order.clear()
                m = n + NWR
                for p in range(SLOTS):
                    scan_slot(n, p)
                    if p == 1:
                        project_x(n, 2)
                        project_x(n, 3)
                    if p == 6:
                        steps(n, 3)
                    if p == 7:
                        pe.wait_ge(S["h0_made"], n + 1)
                        one(sides, "center", n, w("cen96", C), h0[:, :], C)
                    if p == 9:
                        steps(n, 4)
                        wait_read(pe, sides, "center", n)
                        one(sides, "var", n, w("one96", C), sq[:, :], C)
                    if p == 12:
                        steps(n, 5)
                    finish(sides, n, n, p)
                    if p == 13:
                        pe.wait_ge(S["xn_made"], n + 1)
                        in_project(n, 0)
                        in_project(n, 1)
                    if p == 14:
                        in_project(n, 2)
                        in_project(n, 3)
                    if p == 15:
                        wait_read(pe, sides, "inA", n)
                        window_conv(n, "convA", diagA, xpA)
                    if p == 17:
                        wait_read(pe, sides, "inB", n)
                        window_conv(n, "convB", diagB, xpB)
                    if p % 7 in (3, 4) and p < 35:
                        up(sides, m, n, p // 7, p % 7 - 3)
                    if p == 28:
                        project_x(n, 0)
                        project_x(n, 1)
                    if p == 31:
                        steps(n, 0)
                    if p == 34:
                        steps(n, 1)
                    if p == 37:
                        steps(n, 2)
                    if p == 44:
                        down(sides, m, n)
                assert order == [x for x, _, _ in SIDE]

            def last(f):
                c_and_sum(f, 0)
                c_and_sum(f, 1)
                c_and_sum(f, 2)
                for p in (5, 7, 12):
                    finish(sides_f, f, 0, p)

            pe.wait_ge(S["packed"], 16)
            for j in range(4):
                ins = mm(psY[:, 0, j:j + 1], w("inw", C, 128 * j, 128), w("lnb", C), start=True, stop=True)
            ins.then_inc(S["inw_done"], 1)
            pe.wait_ge(S["zeroed_a"], 1)
            pe.wait_ge(S["zeroed_b"], 1)
            mm(psY[:, 1, 0:NP], w("ident"), ysA, start=True, stop=False)
            pe.wait_ge(S["folded_ready"], 1)
            over_chunks(pe, l0_only, lambda b: None, iteration, last)

        @block.scalar
        def _(act):
            do = nc.scalar.activation

            def up_read(ph, m, n, t, half):
                name = f"up{t}_{half}"
                act.wait_ge(S["taps"], 9 * MT * m)
                wait_side(act, ph, name, n)
                R = rows_of(t)
                do(mid[0:R, t, 5 * half:5 * half + 5, 1:HW + 1],
                   side_ps(ph, name, HH, R).rearrange("p (r c) -> p r c", c=HW), ACT.Relu,
                   bias=o1[0:R, t:t + 1], scale=s1[0:R, t:t + 1]).then_inc(side_read[ph.bank(name)], 1)

            def depthwise_read(m, t):
                R = rows_of(t)
                act.wait_ge(S["taps"], 9 * MT * m + 9 * t + 9)
                do(z2[0:R, t, :], acc[0:R, t % 2, :], ACT.Relu, bias=o2[0:R, t:t + 1],
                   scale=s2[0:R, t:t + 1]).then_inc(S["z2_made"], 1)

            def down_read(ph, m, n):
                act.wait_ge(S["x1_made"], m)
                wait_side(act, ph, "down", n)
                do(y3[:, :], side_ps(ph, "down", NP, C), ACT.Identity, bias=o3[0:C, :],
                   scale=s3[0:C, :]).then_inc(side_read[ph.bank("down")], 1)

            def sigmoid_tail(buf, ready, ln_made, made, n):
                act.wait_ge(ready, n + 1)
                do(buf, buf, ACT.Ln).then_inc(ln_made, 1)
                act.wait_ge(ln_made, n + 1)
                do(buf, buf, ACT.Exp, scale=-1.0).then_inc(made, 1)

            def hi_parts(n, k):
                name = f"xp{k}"
                wait_side(act, sides, name, n)
                do(Q[:, k, :], side_ps(sides, name), ACT.Copy)
                do(Fk[:, k % 2, :], side_ps(sides, name, NP, 64), ACT.Copy).then_inc(S["f_made"], 1)

            def mid_part(n, k):
                wait_read(act, sides, f"xp{k}", n)
                do(Q[64:128, k, :], rest[64:128, k % 2, :], ACT.Copy).then_inc(S["q_mid"], 1)

            def step_abs(n, t):
                i, name = DT_TURN[t] % 2, f"dt{t}"
                act.wait_ge(S["delta_made"], 6 * n + DT_TURN[t] - 1 + CREDIT["delta_made"])
                wait_side(act, sides, name, n)
                do(dta_[:, i, :], side_ps(sides, name), ACT.Abs, bias=w("dtb", 128, t, 1)).then_inc(S["abs_made"], 1)
                do(dtm_[:, i, :], side_ps(sides, name), ACT.Relu, bias=w("dtb", 128, t, 1))\
                    .then_inc(side_read[sides.bank(name)], 1)

            def step_exp(n, t):
                i = DT_TURN[t] % 2
                act.wait_ge(S["abs_made"], 6 * n + DT_TURN[t] + 1)
                do(dte[:, i, :], dta_[:, i, :], ACT.Exp, scale=-1.0).then_inc(S["exp_made"], 1)

            def step_log(n, t):
                i = DT_TURN[t] % 2
                act.wait_ge(S["exp_made"], 6 * n + DT_TURN[t] + 1)
                do(dtl[:, i, :], dte[:, i, :], ACT.Ln, bias=1.0).then_inc(S["log_made"], 1)

            def scan_slot(n, p):
                s = SLOTS * n + p
                t, n0 = p // PAIRS, 2 * (p % PAIRS)
                act.wait_ge(S["b_bcast"], s + 1)
                act.wait_ge(S["dbu_made"], s + 1)
                do(Bsb[:, p % 2, :].rearrange("p (j f) -> p j f", j=2), psB[:, :, 0:NP], ACT.Copy)\
                    .then_inc(S["b_evac"], 1)
                if p % PAIRS == 0:
                    act.wait_ge(S["delta_made"], 6 * n + t)
                act.wait_ge(S["scanned"], s + 1)
                back = int(t >= 3)
                keep = slice(0, WP - 1) if back else slice(1, WP)
                src = delta[:, t, :].rearrange("p (w q) -> p w q", q=WP)[:, :, keep]
                for j in range(2):
                    dst = dA[:, p % 2, back + NP * j:back + NP * j + NP].rearrange("p (w q) -> p w q", q=WP)[:, :, keep]
                    ins = do(dst, src, ACT.Exp, scale=A[:, NS * t + n0 + j:NS * t + n0 + j + 1])
                ins.then_inc(S["da_made"], 1)

            def finish(ph, f, n, p):
                if p == 6:
                    for a, (name, R) in enumerate((("cenA", 128), ("cenB", DB))):
                        wait_side(act, ph, name, n)
                        do(cY[0:R, a, :], side_ps(ph, name, NP, R), ACT.Copy)
                        do(sY[0:R, a, :], side_ps(ph, name, NP, R), ACT.Square).then_inc(side_read[ph.bank(name)], 1)
                if p == 8:
                    wait_side(act, ph, "varY", n)
                    do(rY, side_ps(ph, "varY"), ACT.Ln, bias=sb_eps[:, 0:1]).then_inc(side_read[ph.bank("varY")], 1)
                    wait_read(act, ph, "varY", n)
                    do(rY, rY, ACT.Exp, scale=-0.5).then_inc(S["ry_made"], 1)
                if p == 13:
                    wait_side(act, ph, "outp", n)
                    act.wait_ge(S["out_made"], f)
                    do(outs[:, :], side_ps(ph, "outp", NP, C), ACT.Copy).then_inc(side_read[ph.bank("outp")], 1)

            def l0_only(m, r):
                for t in range(MT + 1):
                    if t < MT:
                        up_read(sides_l0, m, m, t, 0)
                        up_read(sides_l0, m, m, t, 1)
                    if t > 0:
                        depthwise_read(m, t - 1)
                down_read(sides_l0, m, m)

            def boundary(b):
                act.wait_ge(S["aggregated"], b + 1)
                do(coef[:, 0:1], meanvar[:, 1:2], ACT.Ln, bias=sb_eps[0:C, 0:1]).then_inc(S["rstd_ln"], 1)
                act.wait_ge(S["rstd_ln"], b + 1)
                do(coef[:, 0:1], coef[:, 0:1], ACT.Exp, scale=-0.5).then_inc(S["rstd_made"], 1)

            def iteration(n, b, r):
                m = n + NWR
                for p in range(SLOTS):
                    scan_slot(n, p)
                    if p == 2:
                        hi_parts(n, 2)
                        hi_parts(n, 3)
                    if p == 4:
                        mid_part(n, 2)
                        mid_part(n, 3)
                    if p == 3:
                        act.wait_ge(S["x1_loaded"], 16 * n + 16)
                        act.wait_ge(S["coef_made"], b + 1)
                        do(v[:, :], x1r[:, :], ACT.Identity, bias=coef[:, 3:4], scale=coef[:, 1:2]).then_inc(S["v_made"], 1)
                        act.wait_ge(S["v_made"], n + 1)
                        do(sigh[:, :], v[:, :], ACT.Exp, scale=-1.0).then_inc(S["eh_made"], 1)
                    if p == 5:
                        sigmoid_tail(sigh[:, :], S["e1h_made"], S["lh_made"], S["sgh_made"], n)
                    finish(sides, n, n, p)
                    if p == 8:
                        wait_side(act, sides, "center", n)
                        do(cen[:, :], side_ps(sides, "center", NP, C), ACT.Copy)
                        do(sq[:, :], side_ps(sides, "center", NP, C), ACT.Square).then_inc(side_read[sides.bank("center")], 1)
                    if p == 10:
                        wait_side(act, sides, "var", n)
                        do(sq[:, :], side_ps(sides, "var", NP, C), ACT.Ln, bias=sb_eps[0:C, 0:1])\
                            .then_inc(side_read[sides.bank("var")], 1)
                        wait_read(act, sides, "var", n)
                        do(sq[:, :], sq[:, :], ACT.Exp, scale=-0.5).then_inc(S["rs_made"], 1)
                    if p == 14:
                        for name, j, xp in (("inA", 0, xpA), ("inB", 1, xpB)):
                            wait_side(act, sides, name, n)
                            do(xp[:, :, 1:WS + 1, 1:WS + 1], win(side_ps(sides, name)), ACT.Identity,
                               bias=inbias[:, j:j + 1]).then_inc(side_read[sides.bank(name)], 1)
                    if p == 15:
                        for name, j in (("inZA", 0), ("inZB", 1)):
                            wait_side(act, sides, name, n)
                            do(vz[:, j, :], side_ps(sides, name), ACT.Identity, bias=inbias[:, 2 + j:3 + j])\
                                .then_inc(side_read[sides.bank(name)], 1)
                    if p == 16:
                        wait_read(act, sides, "inZA", n)
                        wait_read(act, sides, "inZB", n)
                        do(sigz[:, :, :], vz[:, :, :], ACT.Exp, scale=-1.0).then_inc(S["ez_made"], 1)
                    for q, name, j, cb in ((16, "convA", 0, "cba"), (18, "convB", 1, "cbb")):
                        if p == q:
                            wait_side(act, sides, name, n)
                            do(vu[:, j, :], side_ps(sides, name), ACT.Identity, bias=w(cb))\
                                .then_inc(side_read[sides.bank(name)], 1)
                    if p == 18:
                        sigmoid_tail(sigz[:, :, :], S["e1z_made"], S["lz_made"], S["sgz_made"], n)
                    if p == 19:
                        wait_read(act, sides, "convA", n)
                        wait_read(act, sides, "convB", n)
                        do(sigu[:, :, :], vu[:, :, :], ACT.Exp, scale=-1.0).then_inc(S["eu_made"], 1)
                    if p == 21:
                        sigmoid_tail(sigu[:, :, :], S["e1u_made"], S["lu_made"], S["sgu_made"], n)
                    if p == 28:
                        act.wait_ge(S["u_made"], n + 1)
                        do(turned(uM[DB:128]), win(vu[DB:128, 1, :]), ACT.Copy).then_inc(S["um_made"], 1)
                    if p == 29:
                        hi_parts(n, 0)
                        hi_parts(n, 1)
                    if p == 31:
                        mid_part(n, 0)
                        mid_part(n, 1)
                    for t, q in DT_SLOT.items():
                        if p == q + 1:
                            step_abs(n, t)
                        if p == q + 2:
                            step_exp(n, t)
                        if p == q + 3:
                            step_log(n, t)
                    if p % 7 in (4, 5) and p < 36:
                        up_read(sides, m, n, p // 7, p % 7 - 4)
                    if p in (15, 22, 29, 36, 43):
                        depthwise_read(m, p // 7 - 2)
                    if p == 45:
                        down_read(sides, m, n)

            def last(f):
                for p in (6, 8, 13):
                    finish(sides_f, f, 0, p)

            nc.scalar.preload_act_table_set("natural_log_exp_and_others")
            act.wait_ge(S["packed"], 16)
            act.wait_ge(S["zeroed_a"], 1)
            act.wait_ge(S["zeroed_b"], 1)
            act.sem_inc(S["z2_made"], CREDIT["z2_made"])
            for i, (dst, src, R) in enumerate(((s1, "v1", 128), (s2, "v2", 128), (s3, "v3", C))):
                do(dst[0:R, :], w(src, R), ACT.Ln, bias=sb_eps[0:R, 0:1]).then_inc(S["bn_ln"], 1)
                act.wait_ge(S["bn_ln"], i + 1)
                do(dst[0:R, :], dst[0:R, :], ACT.Exp, scale=-0.5).then_inc(S["bn_rs"], 1)
            do(A[:, :], w("alog"), ACT.Exp).then_inc(S["bn_rs"], 1)
            act.wait_ge(S["inw_done"], 1)
            do(inbias[:, :], psY[:, 0, 0:4], ACT.Copy).then_inc(S["inb"], 1)
            act.wait_ge(S["inb"], 1)
            act.wait_ge(S["folded_ready"], 1)
            over_chunks(act, l0_only, boundary, iteration, last)

        @block.vector
        def _(dve):
            V = nc.vector

            def tap(m, t, k):
                R = rows_of(t)
                done = 9 * MT * m + 9 * t + k
                src = mid[0:R, t, k // 3:k // 3 + WS, k % 3:k % 3 + HW]
                dst = acc[0:R, t % 2, :].rearrange("p (r c) -> p r c", c=HW)
                wk = w("wd", R, 9 * t + k, 1)
                if k == 0:
                    dve.wait_ge(S["mid_masked"], MT * m + t + 1)
                    dve.wait_ge(S["z2_made"], MT * m + t - 1 + CREDIT["z2_made"])
                    V.tensor_scalar(dst, src, wk, None, ALU.mult).then_inc(S["taps"], 1)
                else:
                    dve.wait_ge(S["taps"], done)
                    V.scalar_tensor_tensor(out=dst, in0=src, scalar=wk, in1=dst, op0=ALU.mult, op1=ALU.add)\
                        .then_inc(S["taps"], 1)

            def stat(m, r):
                dve.wait_ge(S["x1_made"], m + 1)
                V.bn_stats(stats[:, bass.ds(r * 6, 6)], x1o[:, :]).then_inc(S["stats_made"], 1)

            def cap_and_one(buf, ready, made, n):
                dve.wait_ge(ready, n + 1)
                V.tensor_scalar(buf, buf, EXP_CAP, 1.0, ALU.min, ALU.add).then_inc(made, 1)

            def rests(n, k):
                name = f"xp{k}"
                dve.wait_ge(S["f_made"], 4 * n + (k + 2) % 4 + 1)
                V.tensor_tensor(rest[64:128, k % 2, :], side[64:128, sides.bank(name), 0:NP], Q[64:128, k, :],
                                ALU.subtract).then_inc(side_read[sides.bank(name)], 1)

            def lo_part(n, k):
                dve.wait_ge(S["q_mid"], 4 * n + (k + 2) % 4 + 1)
                V.tensor_tensor(Q[96:128, k, :], rest[96:128, k % 2, :], Q[96:128, k, :], ALU.subtract)\
                    .then_inc(S["q_lo"], 1)

            def log_select(n, t):
                i, turn = DT_TURN[t] % 2, 6 * n + DT_TURN[t]
                dve.wait_ge(S["log_made"], turn + 1)
                V.scalar_tensor_tensor(out=dtl[:, i, :], in0=dte[:, i, :], scalar=LN_SMALL, in1=dtl[:, i, :],
                                       op0=ALU.is_ge, op1=ALU.mult).then_inc(S["logsel_made"], 1)

            def log_max(n, t):
                i, turn = DT_TURN[t] % 2, 6 * n + DT_TURN[t]
                dve.wait_ge(S["logsel_made"], turn + 1)
                dve.wait_ge(S["poly_made"], turn + 1)
                V.tensor_tensor(dtl[:, i, :], dtl[:, i, :], dtp[:, i, :], ALU.max).then_inc(S["logmax_made"], 1)

            def step_size(n, t):
                i, turn = DT_TURN[t] % 2, 6 * n + DT_TURN[t]
                dve.wait_ge(S["logmax_made"], turn + 1)
                V.tensor_tensor(delta[:, t, :], dtl[:, i, :], dtm_[:, i, :], ALU.add).then_inc(S["delta_made"], 1)

            def scan_slot(n, p):
                s = SLOTS * n + p
                back = int(p // PAIRS >= 3)
                dve.wait_ge(S["da_made"], s + 1)
                dve.wait_ge(S["dbu_made"], s + 1 + CREDIT["dbu_made"])
                dve.wait_ge(S["cmult"], s - 1 + CREDIT["cmult"])
                step = -1 if back else 1
                V.tensor_tensor_scan(h[:, p % 3, ::step], dA[:, p % 2, back:back + 2 * NP][:, ::step], dBu[:, p % 2, ::step],
                                     0.0, ALU.mult, ALU.add).then_inc(S["scanned"], 1)
                times_c(n, p)

            def times_c(n, p):
                s = SLOTS * n + p
                q = (p - 1) % SLOTS
                dve.wait_ge(S["c_bcast"], s + 2)
                dve.wait_ge(S["scanned"], s + CREDIT["scanned"])
                dve.wait_ge(S["reduced"], s + 1)
                V.tensor_tensor(hC[:, q % 2, :].rearrange("p (j f) -> p j f", j=2),
                                h[:, q % 3, :].rearrange("p (j f) -> p j f", j=2), psC[:, :, 0:NP],
                                ALU.mult).then_inc(S["cmult"], 1)

            def take_y(n, t, turn):
                p = (PAIRS * t + PAIRS + 2) % SLOTS
                dve.wait_ge(S["reduced"], SLOTS * n + p + 1)
                y = psY[:, t % 2, 0:NP]
                if t == 0:
                    ins = V.scalar_tensor_tensor(out=ysA, in0=uA, scalar=Dm[:, 0:1], in1=y, op0=ALU.mult, op1=ALU.add)
                elif t == 1:
                    ins = V.tensor_copy(ysAT, y)
                elif t == 2:
                    ins = V.scalar_tensor_tensor(out=ysM, in0=uM, scalar=Dm[:, 1:2], in1=y, op0=ALU.mult, op1=ALU.add)
                else:
                    ys = (ysA, ysAT, ysM)[t - 3]
                    ins = V.tensor_tensor(ys, ys, y, ALU.add)
                ins.then_inc(S["y_evac"], 1)

            def finish(f, p):
                parts = ((0, 128, "oga", "oba"), (1, DB, "ogb", "obb"))
                if p == 9:
                    dve.wait_ge(S["ry_made"], f + 1)
                    for a, R, g, _ in parts:
                        ins = V.scalar_tensor_tensor(out=cY[0:R, a, :], in0=cY[0:R, a, :], scalar=w(g, R),
                                                     in1=rY[0:R, :], op0=ALU.mult, op1=ALU.mult)
                    ins.then_inc(S["norm_made"], 1)
                if p == 10:
                    dve.wait_ge(S["norm_made"], f + 1)
                    dve.wait_ge(S["rotated"], 32 * f)
                    for a, R, _, o in parts:
                        ins = V.scalar_tensor_tensor(out=cY[0:R, a, :], in0=cY[0:R, a, :], scalar=w(o, R),
                                                     in1=gateF[0:R, a, :], op0=ALU.add, op1=ALU.mult)
                    ins.then_inc(S["gated"], 1)

            def l0_only(m, r):
                for t in range(MT):
                    for k in range(9):
                        tap(m, t, k)
                stat(m, r)

            def boundary(b):
                wait_apart(dve, S["stats_made"], NWR * (b + 1))
                V.bn_aggr(meanvar[:, :], stats[:, :].rearrange("p (r s) -> p r s", s=6)).then_inc(S["aggregated"], 1)
                dve.wait_ge(S["rstd_made"], b + 1)
                V.tensor_tensor(coef[:, 1:2], coef[:, 0:1], w("gamma", C), ALU.mult).then_inc(S["scale_made"], 1)
                dve.wait_ge(S["scale_made"], 2 * b + 1)
                V.tensor_tensor(coef[:, 2:3], coef[:, 1:2], meanvar[:, 0:1], ALU.mult).then_inc(S["scale_made"], 1)
                dve.wait_ge(S["scale_made"], 2 * b + 2)
                V.tensor_tensor(coef[:, 3:4], w("beta", C), coef[:, 2:3], ALU.subtract).then_inc(S["coef_made"], 1)

            def iteration(n, b, r):
                m = n + NWR
                for p in range(SLOTS):
                    t, at = divmod(p - 6, 7)
                    if 0 <= t < MT and at < 2:
                        tap(m, t, 2 * at)
                    late_tap = (t, 2 * at + 1 if at < 2 else at + 2) if 0 <= t < MT else None
                    if p == 3:
                        rests(n, 2)
                        rests(n, 3)
                    if p == 30:
                        rests(n, 0)
                        rests(n, 1)
                    scan_slot(n, p)
                    if p == 2:
                        take_y(n, 5, 0)
                    if p % PAIRS == 2 and p > 2:
                        take_y(n, p // PAIRS - 1, p // PAIRS)
                    if p == 5:
                        lo_part(n, 2)
                        lo_part(n, 3)
                    if p == 4:
                        cap_and_one(sigh[:, :], S["eh_made"], S["e1h_made"], n)
                    finish(n, p)
                    if p == 17:
                        cap_and_one(sigz[:, :, :], S["ez_made"], S["e1z_made"], n)
                    if p == 20:
                        cap_and_one(sigu[:, :, :], S["eu_made"], S["e1u_made"], n)
                    if p == 27:
                        dve.wait_ge(S["sgu_made"], n + 1)
                        dve.wait_ge(S["y_evac"], 6 * n + 4)
                        V.tensor_tensor(uA, vu[:, 0, :], sigu[:, 0, :], ALU.mult)
                        V.tensor_tensor(uM[0:DB], vu[0:DB, 1, :], sigu[0:DB, 1, :], ALU.mult)
                        V.tensor_tensor(vu[DB:128, 1, :], vu[DB:128, 1, :], sigu[DB:128, 1, :], ALU.mult)\
                            .then_inc(S["u_made"], 1)
                    if p == 32:
                        lo_part(n, 0)
                        lo_part(n, 1)
                    for t, q in DT_SLOT.items():
                        if p == q + 4:
                            log_select(n, t)
                        if p == q + 5:
                            log_max(n, t)
                        if p == q + 6:
                            step_size(n, t)
                    if late_tap is not None:
                        tap(m, *late_tap)
                    if p == 47:
                        stat(m, r)

            def last(f):
                times_c(f, 0)
                take_y(f, 5, 0)
                finish(f, 9)
                finish(f, 10)

            V.memset(Z[:, 0:len_a], 0.0).then_inc(S["zeroed_a"], 1)
            dve.wait_ge(S["packed"], 16)
            dve.wait_ge(S["zeroed_b"], 1)
            dve.sem_inc(S["scanned"], CREDIT["scanned"])
            dve.sem_inc(S["cmult"], CREDIT["cmult"])
            dve.sem_inc(S["delta_made"], CREDIT["delta_made"])
            V.tensor_copy(sel[:, :, :], w("selcol").unsqueeze(2).to_broadcast([128, 32, 128]))
            for tapk in range(9):
                V.tensor_scalar(diagA[:, tapk, :], w("ident"), w("cwa", 128, tapk, 1), None, ALU.mult)
                V.tensor_scalar(diagB[:, tapk, :], w("ident"), w("cwb", 128, tapk, 1), None, ALU.mult)
            V.reduce_sum(Dm[:, 0:1], w("dsa"), axis=mybir.AxisListType.X)
            V.reduce_sum(Dm[:, 1:2], w("dsm"), axis=mybir.AxisListType.X)
            dve.wait_ge(S["bn_rs"], 4)
            V.tensor_scalar(A[:, :], A[:, :], -1.0, None, ALU.mult)
            bns = ((s1, o1, "1", 128), (s2, o2, "2", 128), (s3, o3, "3", C))
            for s_, o_, i, R in bns:
                ins = V.tensor_tensor(s_[0:R, :], s_[0:R, :], w("g" + i, R), ALU.mult)
            ins.then_inc(S["folded_bn"], 1)
            dve.wait_ge(S["folded_bn"], 1)
            for s_, o_, i, R in bns:
                ins = V.tensor_tensor(o_[0:R, :], s_[0:R, :], w("m" + i, R), ALU.mult)
            ins.then_inc(S["folded_bn"], 1)
            dve.wait_ge(S["folded_bn"], 2)
            for s_, o_, i, R in bns:
                ins = V.tensor_tensor(o_[0:R, :], w("b" + i, R), o_[0:R, :], ALU.subtract)
            dve.wait_ge(S["inw_done"], 1)
            V.tensor_scalar(w("inw", C), w("inw", C), w("lng", C), None, ALU.mult)
            V.tensor_scalar(w("owa"), w("owa"), w("alpha"), None, ALU.mult)
            V.tensor_scalar(w("owb", DB), w("owb", DB), w("alpha", DB), None, ALU.mult).then_inc(S["folded_ready"], 1)
            dve.wait_ge(S["folded_ready"], 1)
            over_chunks(dve, l0_only, boundary, iteration, last)

        @block.gpsimd
        def _(pool):
            G = nc.gpsimd

            def mask_rows(ph, m, n, r, t):
                for half in range(2):
                    name = f"up{t}_{half}"
                    wait_apart(pool, side_read[ph.bank(name)], ph.fills(name, n))
                R = rows_of(t)
                for side_, row in ((0, 0), (1, XP - 1)):
                    edge = mid[0:R, t, row, 1:HW + 1]
                    ins = G.tensor_tensor(edge, edge, masks[0:R, bass.ds((r * 2 + side_) * HW, HW)], ALU.mult)
                ins.then_inc(S["mid_masked"], 1)

            def residual_l0(ph, m, n):
                wait_read(pool, ph, "down", n)
                pool.wait_ge(S["x1_stored"], 16 * m)
                pool.wait_ge(S["stats_made"], m)
                pool.wait_ge(S["x_loaded"], 16 * m + 16)
                G.tensor_tensor(win(x1o[:, :]), image_rows(y3[:, :]), image_rows(xin[:, HW:HW + NP]), ALU.add)\
                    .then_inc(S["x1_made"], 1)

            def poly(n, t):
                i, turn = DT_TURN[t] % 2, 6 * n + DT_TURN[t] + 1
                wait_apart(pool, S["exp_made"], turn)
                G.tensor_scalar(dtp[:, i, :], dte[:, i, :], -0.5, 1.0, ALU.mult, ALU.add).then_inc(S["poly0_made"], 1)
                pool.wait_ge(S["poly0_made"], turn)
                G.tensor_tensor(dtp[:, i, :], dtp[:, i, :], dte[:, i, :], ALU.mult).then_inc(S["poly_made"], 1)

            def step_u(n, t):
                pool.wait_ge(S["delta_made"], 6 * n + DT_TURN[t] + 1 + CREDIT["delta_made"])
                G.tensor_tensor(dtu[:, t, :], delta[:, t, :], (uA, uAT, uM)[t % 3], ALU.mult).then_inc(S["dtu_made"], 1)

            def scan_slot(n, p):
                s = SLOTS * n + p
                t = p // PAIRS
                if p % PAIRS == 0:
                    pool.wait_ge(S["dtu_made"], 6 * n + t)
                pool.wait_ge(S["b_evac"], s + 1)
                pool.wait_ge(S["scanned"], s + 1)
                G.tensor_tensor(dBu[:, p % 2, :].rearrange("p (j f) -> p j f", j=2),
                                Bsb[:, p % 2, :].rearrange("p (j f) -> p j f", j=2),
                                dtu[:, t, :].unsqueeze(1).to_broadcast([128, 2, NP]), ALU.mult).then_inc(S["dbu_made"], 1)

            def finish(ph, f, n, p):
                if p == 3:
                    pool.wait_ge(S["y_evac"], 6 * f + 1)
                    G.tensor_tensor(win(yAs), win(ysA), turned(ysAT), ALU.add).then_inc(S["yas_made"], 1)
                if p == 14:
                    wait_read(pool, ph, "outp", n)
                    pool.wait_ge(S["rotated"], 32 * f)
                    pool.wait_ge(S["out_stored"], 16 * f)
                    G.tensor_tensor(outb[:, :], outs[:, :], residF[0:C, :], ALU.add).then_inc(S["out_made"], 1)

            def l0_only(m, r):
                for t in range(MT):
                    mask_rows(sides_l0, m, m, r, t)
                residual_l0(sides_l0, m, m)

            def iteration(n, b, r):
                m = n + NWR
                for p in range(SLOTS):
                    scan_slot(n, p)
                    finish(sides, n, n, p)
                    if p == 6:
                        pool.wait_ge(S["sgh_made"], n + 1)
                        G.tensor_tensor(h0[:, :], v[:, :], sigh[:, :], ALU.mult).then_inc(S["h0_made"], 1)
                    if p == 11:
                        pool.wait_ge(S["rs_made"], n + 1)
                        G.tensor_tensor(sq[:, :], cen[:, :], sq[:, :], ALU.mult).then_inc(S["xn_made"], 1)
                    if p == 21:
                        pool.wait_ge(S["sgz_made"], n + 1)
                        pool.wait_ge(S["rotated"], 32 * n + 32)
                        G.tensor_tensor(gateP[:, :, :], vz[:, :, :], sigz[:, :, :], ALU.mult).then_inc(S["gate_made"], 1)
                    if p == 22:
                        wait_apart(pool, S["h0_made"], n + 1)
                        G.tensor_scalar(v[:, :], h0[:, :], w("alpha", C), 0.0, ALU.mult, ALU.add).then_inc(S["alphah_made"], 1)
                        pool.wait_ge(S["alphah_made"], n + 1)
                        G.tensor_tensor(residP[0:C, :], v[:, :], x1r[:, :], ALU.add).then_inc(S["resid_made"], 1)
                    if p == 27:
                        pool.wait_ge(S["y_evac"], 6 * n + 4)
                        pool.wait_ge(S["sgu_made"], n + 1)
                        G.tensor_tensor(turned(uAT), win(vu[:, 0, :]), win(sigu[:, 0, :]), ALU.mult).then_inc(S["ut_made"], 1)
                    for t, q in DT_SLOT.items():
                        if p == q + 3:
                            poly(n, t)
                        if p == q + 7:
                            step_u(n, t)
                    if p % 7 == 5 and p < 35:
                        mask_rows(sides, m, n, r, p // 7)
                    if p == 46:
                        residual_l0(sides, m, n)

            def last(f):
                finish(sides_f, f, 0, 3)
                finish(sides_f, f, 0, 14)

            G.memset(Z[:, len_a:], 0.0)
            G.memset(sb_eps[:, :], EPS).then_inc(S["zeroed_b"], 1)
            pool.sem_inc(S["dbu_made"], CREDIT["dbu_made"])
            pool.sem_inc(S["dtu_made"], CREDIT["dtu_made"])
            pool.wait_ge(S["zeroed_a"], 1)
            pool.wait_ge(S["masks_in"], 16)
            pool.wait_ge(S["folded_ready"], 1)
            over_chunks(pool, l0_only, lambda b: None, iteration, last)


def kernel(**inputs):
    import concourse.bacc as bacc
    from concourse.bass_utils import run_bass_kernel_spmd

    f = {k: np.asarray(a, dtype=a.dtype) for k, a in inputs.items()}
    x = f["x"]
    xp = np.pad(x, ((0, 0), (0, 0), (1, 1), (0, 0)))
    x_dev = np.zeros((CHUNKS + 1 + NWR, C, HALO), x.dtype)
    for r in range(NWR):
        x_dev[r:CHUNKS:NWR] = xp[:, :, WS * r:WS * r + WS + 2, :].reshape(B, C, HALO)

    cols = {}

    def put(name, a):
        a = a.reshape(a.shape[0], -1)
        full = np.zeros((128, COL[name][1]), np.float32)
        full[:a.shape[0], :a.shape[1]] = a
        cols[name] = full

    def by_tile(a):
        a = a.reshape(E6, -1)
        a = np.concatenate([a, np.zeros((MT * 128 - E6, a.shape[1]), a.dtype)])
        return a.reshape(MT, 128, -1).transpose(1, 0, 2).reshape(128, -1)

    put("w1", f["L0_conv_w1"].reshape(E6, C).T)
    put("w3", by_tile(f["L0_conv_w3"].reshape(C, E6).T))
    put("wd", by_tile(f["L0_conv_wd"].reshape(E6, 9)))
    for i in "12":
        for a in "gbm":
            put(a + i, by_tile(f[f"L0_conv_{a}{i}"]))
        var = by_tile(f["L0_conv_v" + i])
        var[E6 - 128 * (MT - 1):, MT - 1] = 1.0
        put("v" + i, var)
    for a in "gbmv":
        put(a + "3", f[f"L0_conv_{a}3"])
    L1 = {k[8:]: a for k, a in f.items() if k.startswith("L1_conv_")}
    put("gamma", L1["gamma"])
    put("beta", L1["beta"])
    put("alpha", np.broadcast_to(L1["alpha"], (128, 1)))
    put("lng", L1["ln1_g"])
    put("lnb", L1["ln1_b"])
    iw = L1["in_proj_w"]
    hi, zhi = iw[:, 128:DN], iw[:, DN + 128:]
    put("inw", np.concatenate([iw[:, :128], hi, hi, iw[:, DN:DN + 128], zhi, zhi], 1))
    cw, cb = L1["conv_w"].reshape(DN, 9), L1["conv_b"]
    put("cwa", cw[:128])
    put("cwb", np.concatenate([cw[128:], cw[128:]]))
    put("cba", cb[:128])
    put("cbb", np.concatenate([cb[128:], cb[128:]]))
    xw = L1["x_proj_w"]
    rows = np.zeros((K, 128, DN), np.float32)
    for at in (0, 64, 96):
        rows[:, at:at + 2 * NS] = xw[:, DTR:]
    rows[:, 32:32 + DTR] = xw[:, :DTR]
    put("xpa", rows[:, :, :128].transpose(2, 0, 1))
    put("xpb", np.concatenate([rows[0::2, :, 128:], rows[1::2, :, 128:]], 2).transpose(2, 0, 1))
    dw = np.zeros((64, K, DN), np.float32)
    dw[32:32 + DTR] = L1["dt_w"].transpose(2, 0, 1)
    put("dta", dw[:, :, :128])
    put("dtm", dw[:, :, 128:])

    def by_scan_tile(a):
        a = a.reshape(K, DN, -1)
        mixed = [np.concatenate([a[k, 128:], a[k + 1, 128:]]) for k in (0, 2)]
        return np.stack([a[0, :128], a[1, :128], mixed[0], a[2, :128], a[3, :128], mixed[1]], 1)

    put("dtb", by_scan_tile(L1["dt_b"]))
    put("alog", by_scan_tile(L1["A_logs"]))
    ds = L1["Ds"].reshape(K, DN).T
    put("dsa", ds[:128])
    put("dsm", ds[128:])
    put("oga", L1["outnorm_g"][:128])
    put("ogb", L1["outnorm_g"][128:])
    put("oba", L1["outnorm_b"][:128])
    put("obb", L1["outnorm_b"][128:])
    put("owa", L1["out_proj_w"][:128])
    put("owb", L1["out_proj_w"][128:])
    put("cen96", np.eye(C, dtype=np.float32) - np.float32(1 / C))
    put("one96", np.full((C, C), 1 / C, np.float32))
    cen = (np.eye(DN, dtype=np.float32) - np.float32(1 / DN))
    zero = np.zeros((DB, 128), np.float32)
    put("cenaa", cen[:128, :128])
    put("cenalo", np.concatenate([cen[128:, :128], zero]))
    put("cenahi", np.concatenate([zero, cen[128:, :128]]))
    put("cenba", cen[:128, 128:])
    put("cenblo", np.concatenate([cen[128:, 128:], zero[:, :DB]]))
    put("cenbhi", np.concatenate([zero[:, :DB], cen[128:, 128:]]))
    put("one192", np.full((128, 128), 1 / DN, np.float32))
    put("ident", np.eye(128, dtype=np.float32))
    e32 = np.eye(32, dtype=np.float32)
    put("selcol", np.concatenate([e32, 0 * e32, e32, e32]))
    pack = np.concatenate([cols[name] for name, _ in PACK], 1)
    m = np.ones((NWR, 2, HW), np.float32)
    m[0, 0] = 0
    m[NWR - 1, 1] = 0
    mask = np.broadcast_to(m.reshape(1, -1), (128, NWR * 2 * HW)).copy()

    nc = bacc.Bacc("TRN2", target_bir_lowering=False, num_devices=1)
    fp32 = mybir.dt.float32
    ins = {"x_dev": x_dev, "pack": pack, "mask": mask}
    aps = {k: nc.dram_tensor(k, a.shape, fp32, kind="ExternalInput").ap() for k, a in ins.items()}
    x1_dram = nc.dram_tensor("x1_dram", (CHUNKS + 1 + NWR, C, NP), fp32).ap()
    out = nc.dram_tensor("out", (CHUNKS + 2, C, NP), fp32, kind="ExternalOutput").ap()
    build(nc, aps["x_dev"], aps["pack"], aps["mask"], x1_dram, out)
    got = run_bass_kernel_spmd(nc, [ins], core_ids=[0]).results[0]["out"]
    y = got[2:].reshape(B, NWR, C, NWR, WS, WS).transpose(0, 2, 1, 4, 3, 5)
    return np.ascontiguousarray(y.reshape(B, C, HW, HW))
```

```python
import concourse.bass as bass
from concourse import mybir
from contextlib import ExitStack
import numpy as np

B, C, HW, WS = 32, 96, 56, 8
NWR = HW // WS
NP = WS * HW
WP = WS * WS
HALO = (WS + 2) * HW
HH = HALO // 2
CHUNKS = B * NWR
E6, MT = 6 * C, 5
DN, NS, K, DTR = 2 * C, 16, 4, C // 16
DB = DN - 128
TILES = 6
PAIRS = 8
SLOTS = TILES * PAIRS
XP = WS + 2
EPS = 1e-5
LN_SMALL = 2.0 ** -11
EXP_CAP = 2.0 ** 60


def rows_of(t):
    return min(128, E6 - 128 * t)


PACK = [("w1", E6), ("w3", MT * C), ("wd", MT * 9),
        ("g1", MT), ("b1", MT), ("m1", MT), ("v1", MT), ("g2", MT), ("b2", MT), ("m2", MT), ("v2", MT),
        ("g3", 1), ("b3", 1), ("m3", 1), ("v3", 1),
        ("gamma", 1), ("beta", 1), ("alpha", 1), ("lng", 1), ("lnb", 1), ("inw", 512),
        ("cwa", 9), ("cwb", 6), ("cba", 1), ("cbb", 1),
        ("xpa", K * 128), ("xpb", 2 * 128), ("dta", K * 128), ("dtm", K * DB), ("dtb", TILES),
        ("alog", TILES * NS), ("dsa", K), ("dsm", K), ("oga", 1), ("oba", 1), ("ogb", 1), ("obb", 1),
        ("owa", C), ("owb", C),
        ("cen96", C), ("one96", C), ("cenaa", 128), ("cenalo", 128), ("cenahi", 128),
        ("cenba", DB), ("cenblo", DB), ("cenbhi", DB), ("one192", 128), ("ident", 128), ("twice", 128), ("selcol", 32)]
COL, _at = {}, 0
for _name, _n in PACK:
    COL[_name] = (_at, _n)
    _at += _n
PACKED = _at

SIDE = [("xp2", 2, 4), ("xp3", 2, 4), ("cenA", 5, 6), ("cenB", 5, 6), ("center", 7, 8), ("up0_0", 7, 8),
        ("var", 9, 10), ("up0_1", 9, 10), ("varY", 11, 12), ("dt3", 11, 12), ("inA", 13, 14), ("inB", 13, 14),
        ("up1_0", 15, 16), ("up1_1", 15, 16), ("outp", 17, 18), ("dt4", 17, 18), ("dt5", 19, 20), ("inZA", 21, 22),
        ("inZB", 21, 22), ("up2_0", 23, 24), ("up2_1", 23, 24), ("up3_0", 25, 26), ("up3_1", 25, 26),
        ("up4_0", 27, 28), ("up4_1", 27, 28), ("xp0", 31, 33), ("xp1", 31, 33), ("dt0", 34, 35),
        ("dt1", 36, 37), ("dt2", 39, 40), ("down", 41, 47)]
assert all(SIDE[i][1] > SIDE[i - 2][2] for i in range(2, len(SIDE)))
AT = {name: slot for name, slot, _ in SIDE}
TAPS = {0: (12, 19), 1: (19, 28), 2: (28, 36), 3: (36, 44)}
SHARED = {4: (30, 42)}
DOWN = {0: 41, 1: 42, 2: 43, 4: 44, 3: 46}
assert all(a > AT[f"up{t}_1"] + 2 for t, (a, _) in (TAPS | SHARED).items())


def taps_in(plan, p):
    return [(t, k) for t, (a, e) in plan.items() for k in range(9) if a + k * (e - a) // 9 == p]


TAP_TURN = {t: i for i, t in enumerate(TAPS)}
SHARED_TURN = {t: i for i, t in enumerate(SHARED)}
L0_SIDE = [f"up{t}_{h}" for t in range(MT) for h in range(2)] + ["down"]
ACT_HEAD = 2
F_SIDE = ["cenA", "cenB", "varY", "outp"]
DT_SLOT = {int(name[2:]): slot for name, slot, _ in SIDE if name.startswith("dt")}
DT_TURN = {t: i for i, t in enumerate([3, 4, 5, 0, 1, 2])}


class SideBanks:

    def __init__(self, names, before):
        self.at = {x: (i % 2, i // 2) for i, x in enumerate(names)}
        self.per = [(len(names) + 1) // 2, len(names) // 2]
        self.before = before

    def bank(self, name):
        return self.at[name][0]

    def fills(self, name, n):
        bank, nth = self.at[name]
        return self.before[bank] + nth + 1 + self.per[bank] * n

    def after(self, n):
        return [self.before[i] + self.per[i] * n for i in range(2)]


def build(nc, x_dev, pack, mask, x1_dram, out):
    fp32, bf16 = mybir.dt.float32, mybir.dt.bfloat16
    ALU, ACT = mybir.AluOpType, mybir.ActivationFunctionType
    ctx = ExitStack()
    with ctx:
        def sb(name, shape, dt=fp32):
            return ctx.enter_context(nc.sbuf_tensor(name, shape, dt))

        def sem(name):
            return ctx.enter_context(nc.semaphore(name))

        W = sb("weights", [128, PACKED])

        def w(name, rows=128, a=0, n=None):
            at, width = COL[name]
            return W[0:rows, at + a:at + (width if n is None else a + n)]

        words = [("mid", MT * XP * (HW + 2)), ("xpA", NWR * XP * XP), ("xpB", NWR * XP * XP),
                 ("dA", 2 * (2 * NP + 1)), ("h", 3 * 2 * NP), ("hC", 2 * 2 * NP), ("Q", K * NP // 2), ("uA", NP), ("uAT", NP), ("uM", NP),
                 ("delta", TILES * NP), ("dtu", TILES * NP), ("ysA", NP), ("ysAT", NP), ("ysM", NP),
                 ("gateP", 2 * NP), ("gateF", 2 * NP), ("residP", NP), ("residF", NP)]
        Z = sb("zeroed_once", [128, sum(n for _, n in words)])
        len_a = sum(n for _, n in words) * 2 // 3
        sb_eps = sb("eps", [128, 1])
        z, at = {}, 0
        for name, n in words:
            z[name] = Z[:, at:at + n]
            at += n
        mid = z["mid"].rearrange("p (t r c) -> p t r c", t=MT, r=XP)
        xpA = z["xpA"].rearrange("p (w i j) -> p w i j", w=NWR, i=XP)
        xpB = z["xpB"].rearrange("p (w i j) -> p w i j", w=NWR, i=XP)
        dA = z["dA"].rearrange("p (s f) -> p s f", s=2)
        h = z["h"].rearrange("p (s f) -> p s f", s=3)
        hC = z["hC"].rearrange("p (s f) -> p s f", s=2)
        Q = z["Q"].bitcast(bf16).rearrange("p (k f) -> p k f", k=K)
        uA, uAT, uM = z["uA"], z["uAT"], z["uM"]
        delta = z["delta"].rearrange("p (t f) -> p t f", t=TILES)
        dtu = z["dtu"].rearrange("p (t f) -> p t f", t=TILES)
        ysA, ysAT, ysM = z["ysA"], z["ysAT"], z["ysM"]
        gateP = z["gateP"].rearrange("p (a f) -> p a f", a=2)
        gateF = z["gateF"].rearrange("p (a f) -> p a f", a=2)
        residP, residF = z["residP"], z["residF"]

        sel = sb("sel", [128, 32, 128], bf16)
        diagA = sb("diagA", [128, 9, 128])
        diagB = sb("diagB", [128, 6, 128])
        masks = sb("masks", [128, NWR * 2 * HW])
        A = sb("A", [128, TILES * NS])
        s1, o1 = sb("s1", [128, MT]), sb("o1", [128, MT])
        s2, o2 = sb("s2", [128, MT]), sb("o2", [128, MT])
        s3, o3 = sb("s3", [128, 1]), sb("o3", [128, 1])
        inbias = sb("inbias", [128, 4])
        Dm = sb("Dm", [128, 2])
        xin = sb("xin", [C, HALO])
        z2 = sb("z2", [128, MT, NP])
        product = sb("product", [128, 2, NP])
        y3 = sb("y3", [C, NP])
        x1o = sb("x1o", [C, NP])
        stats = sb("stats", [C, NWR * 6])
        meanvar = sb("meanvar", [C, 2])
        coef = sb("coef", [C, 4])
        x1r = sb("x1r", [C, NP])
        v = sb("v", [C, NP])
        sigh = sb("sigh", [C, NP])
        h0 = sb("h0", [C, NP])
        cen = sb("cen", [C, NP])
        sq = sb("sq", [C, NP])
        vz = sb("vz", [128, 2, NP])
        sigz = sb("sigz", [128, 2, NP])
        vu = sb("vu", [128, 2, NP])
        sigu = sb("sigu", [128, 2, NP])
        Fk = sb("Fk", [64, 2, NP])
        rest = sb("rest", [128, 2, NP])
        dta_, dtm_ = sb("dt_abs", [128, 2, NP]), sb("dt_pos", [128, 2, NP])
        dte, dtl = sb("dt_exp", [128, 2, NP]), dta_
        dtp = sb("dt_poly", [128, 2, NP])
        Bsb = sb("Bsb", [128, 2, 2 * NP])
        dBu = sb("dBu", [128, 2, 2 * NP])
        yAs, rY = sigz[:, 0, :], sigz[:, 1, :]
        cY, sY = vu, sigu
        outs = sb("outs", [C, NP])
        outb = sb("outb", [C, NP])

        psum = ctx.enter_context(nc.psum_tensor("psum", [128, 8, 512], fp32))
        psB, psC, psY, side = psum[:, 0:2, :], psum[:, 2:4, :], psum[:, 4:6, :], psum[:, 6:8, :]

        def win(ap):
            return ap.rearrange("p (w i j) -> p w i j", i=WS, j=WS)

        def turned(ap):
            return ap.rearrange("p (w i j) -> p w j i", i=WS, j=WS)

        def image_rows(ap):
            return ap.rearrange("p (i w j) -> p w i j", i=WS, j=WS)

        names = """packed zeroed_a zeroed_b folded_bn folded_ready ident_ready dsum inw_done seeded bn_ln bn_rs inb
            x_loaded mid_masked taps products shared_sums z2_made x1_made x1_stored stats_made aggregated rstd_ln rstd_made scale_made coef_made
            x1_loaded v_made eh_made e1h_made lh_made sgh_made h0_made lnx_made rs_made xn_made
            vz_made ez_made e1z_made lz_made sgz_made gate_made vu_made eu_made e1u_made lu_made sgu_made
            alphah_made resid_made u_made ut_made um_made conv_made conv_read
            f_made q_mid q_lo abs_made exp_made log_made poly0_made poly_made
            logsel_made logmax_made delta_made dtu_made
            b_bcast b_evac c_bcast da_made dbu_made scanned cmult reduced y_evac
            yas_made sy_made lny_made ry_made norm_made gated outs_made out_made out_stored rotated masks_in""".split()
        S = {x: sem(x) for x in names}
        side_ready = [sem("side_ready0"), sem("side_ready1")]
        side_read = [sem("side_read0"), sem("side_read1")]
        passed = {e: sem(f"passed_{i}") for i, e in enumerate((nc.tensor.engine, nc.vector.engine, nc.gpsimd.engine))}
        CREDIT = {"shared_sums": 1, "scanned": 2, "dbu_made": 2, "cmult": 2, "delta_made": 2, "dtu_made": 2}

        sides_l0 = SideBanks(L0_SIDE, [0, 0])
        sides = SideBanks([x for x, _, _ in SIDE], sides_l0.after(NWR))
        sides_f = SideBanks(F_SIDE, sides.after(CHUNKS + 1))

        def wait_side(eng, ph, name, n):
            eng.wait_ge(side_ready[ph.bank(name)], ph.fills(name, n))

        def wait_read(eng, ph, name, n):
            eng.wait_ge(side_read[ph.bank(name)], ph.fills(name, n))

        def wait_apart(eng, semaphore, value):
            eng.wait_ge(semaphore, value)
            eng.sem_inc(passed[eng.engine], 1)

        def side_ps(ph, name, width=NP, rows=128):
            return side[0:rows, ph.bank(name), 0:width]

        def over_chunks(eng, l0_only, boundary, iteration, last, slots=None):
            with eng.Fori(0, NWR) as r:
                l0_only(r, r)
            if slots:
                slots(0, 0, 0, ACT_HEAD)
            boundary(0)
            with eng.Fori(0, B) as b:
                with eng.Fori(0, NWR) as r:
                    n = eng.snap(b * NWR + r)
                    iteration(n, b, r)
                boundary(b + 1)
            if slots:
                slots(CHUNKS, B, ACT_HEAD, SLOTS)
            else:
                iteration(CHUNKS, B, 0)
            last(CHUNKS + 1)

        block = ctx.enter_context(nc.Block())

        @block.sync
        def _(sp):
            sp.dma_start(W[:, :], pack).then_inc(S["packed"], 16)
            sp.dma_start(masks[:, :], mask).then_inc(S["masks_in"], 16)

            def load_x(m):
                sp.wait_ge(S["x1_made"], m)
                sp.dma_start(xin[:, :], x_dev[bass.ds(m, 1)].rearrange("a c f -> (a c) f")).then_inc(S["x_loaded"], 16)

            def store_x1(m):
                sp.wait_ge(S["x1_made"], m + 1)
                sp.dma_start(x1_dram[bass.ds(m, 1)].rearrange("a c f -> (a c) f"), x1o[:, :]).then_inc(S["x1_stored"], 16)

            def store_out(f):
                sp.wait_ge(S["out_made"], f + 1)
                sp.dma_start(out[bass.ds(f, 1)].rearrange("a c f -> (a c) f"), outb[:, :]).then_inc(S["out_stored"], 16)

            def l0_only(m, r):
                load_x(m)
                store_x1(m)

            def iteration(n, b, r):
                load_x(n + NWR)
                sp.wait_ge(S["x1_stored"], 16 * n + 16)
                sp.wait_ge(S["resid_made"], n)
                sp.dma_start(x1r[:, :], x1_dram[bass.ds(n, 1)].rearrange("a c f -> (a c) f")).then_inc(S["x1_loaded"], 16)
                store_out(n)
                sp.wait_ge(S["gated"], n + 1)
                sp.wait_ge(S["gate_made"], n)
                sp.dma_start(gateF[:, :, :], gateP[:, :, :]).then_inc(S["rotated"], 16)
                sp.dma_start(residF[0:C, :], residP[0:C, :]).then_inc(S["rotated"], 16)
                store_x1(n + NWR)

            def last(f):
                store_out(f)

            sp.wait_ge(S["packed"], 16)
            over_chunks(sp, l0_only, lambda b: None, iteration, last)
            sp.wait_ge(S["x1_stored"], 16 * (CHUNKS + 1 + NWR))
            sp.wait_ge(S["out_stored"], 16 * (CHUNKS + 2))

        @block.tensor
        def _(pe):
            mm = nc.tensor.matmul
            order = []

            def open_side(ph, name, n):
                pe.wait_ge(side_read[ph.bank(name)], ph.fills(name, n) - 1)

            def done_side(ph, name, ins):
                order.append(name)
                ins.then_inc(side_ready[ph.bank(name)], 1)

            def up(ph, m, n, t, half):
                if t == 0 and half == 0:
                    pe.wait_ge(S["x_loaded"], 16 * m + 16)
                name = f"up{t}_{half}"
                open_side(ph, name, n)
                done_side(ph, name, mm(side_ps(ph, name, HH, rows_of(t)), w("w1", C, 128 * t, rows_of(t)),
                                       xin[:, HH * half:HH * half + HH], start=True, stop=True))

            def down(ph, m, n, t):
                turn = list(DOWN).index(t)
                pe.wait_ge(S["z2_made"], MT * m + turn + 1)
                if turn == 0:
                    open_side(ph, "down", n)
                ins = mm(side_ps(ph, "down", NP, C), w("w3", rows_of(t), C * t, C), z2[0:rows_of(t), t, :],
                         start=turn == 0, stop=turn == MT - 1)
                if turn == MT - 1:
                    done_side(ph, "down", ins)

            def project_x(n, k):
                name = f"xp{k}"
                if k == 0:
                    pe.wait_ge(S["u_made"], n + 1)
                if k == 1:
                    pe.wait_ge(S["ut_made"], n + 1)
                    pe.wait_ge(S["um_made"], n + 1)
                open_side(sides, name, n)
                lo, src = (0, uA) if k % 2 == 0 else (DB, uAT)
                mm(side_ps(sides, name), w("xpa", 128, 128 * k, 128), src, start=True, stop=False)
                at = COL["xpb"][0] + 128 * (k // 2)
                done_side(sides, name, mm(side_ps(sides, name), W[lo:lo + DB, at:at + 128], uM[lo:lo + DB, :],
                                          start=False, stop=True))

            def steps(n, t):
                name = f"dt{t}"
                if t in (0, 3):
                    pe.wait_ge(S["f_made"], 4 * n + (2 if t == 3 else 4))
                if t % 3 < 2:
                    open_side(sides, name, n)
                else:
                    wait_apart(pe, side_read[sides.bank(name)], sides.fills(name, n) - 1)
                k0 = 0 if t < 3 else 2
                if t % 3 < 2:
                    k = k0 + t % 3
                    ins = mm(side_ps(sides, name), w("dta", 64, 128 * k, 128), Fk[:, k % 2, :], start=True, stop=True)
                else:
                    ps = side[:, sides.bank(name), 0:NP]
                    mm(ps[0:DB], w("dtm", 64, DB * k0, DB), Fk[:, 0, :], start=True, stop=True)
                    ins = mm(ps[DB:128], w("dtm", 64, DB * (k0 + 1), DB), Fk[:, 1, :], start=True, stop=True)
                done_side(sides, name, ins)

            def one(ph, name, n, lhs, rhs, rows):
                open_side(ph, name, n)
                done_side(ph, name, mm(side_ps(ph, name, NP, rows), lhs, rhs, start=True, stop=True))

            def in_project(n, j):
                name = ("inA", "inB", "inZA", "inZB")[j]
                one(sides, name, n, w("inw", C, 128 * j, 128), sq[:, :], 128)

            def window_conv(n, j, part):
                if part == 0:
                    wait_read(pe, sides, ("inA", "inB")[j], n)
                    pe.wait_ge(S["y_evac"], 6 * n + 2 + j)
                di = part
                taps = [(diagA[:, 3 * di + dj, :], xpA, dj) for dj in range(3)] if j == 0 else \
                    [(diagB[:, 2 * di, :], xpB, 0), (diagB[0:DB, 2 * di + 1, :], xpB[0:DB], 2)]
                for i, (diag, xp, dj) in enumerate(taps):
                    ins = mm(psY[:, j, 0:NP], diag, xp[:, :, di:di + WS, dj:dj + WS],
                             start=part == 0 and i == 0, stop=part == 2 and i == len(taps) - 1)
                if part == 2:
                    ins.then_inc(S["conv_made"], 1)

            def broadcast(p, first_row, ps, done):
                t, n0 = p // PAIRS, 2 * (p % PAIRS)
                k0 = 0 if t < 3 else 2
                for j in range(2):
                    row = first_row + n0 + j
                    if t % 3 < 2:
                        ins = mm(ps[:, j, 0:NP], sel[:, row, :], Q[:, k0 + t % 3, :], start=True, stop=True)
                    else:
                        mm(ps[0:DB, j, 0:NP], sel[:, row, 0:DB], Q[:, k0, :], start=True, stop=True)
                        ins = mm(ps[DB:128, j, 0:NP], sel[:, row, 0:DB], Q[:, k0 + 1, :], start=True, stop=True)
                ins.then_inc(done, 1)

            def scan_slot(n, p):
                s = SLOTS * n + p
                c_rows(n, p)
                if p < SLOTS:
                    if p == 0:
                        pe.wait_ge(S["q_lo"], 4 * n)
                    if p == 24:
                        pe.wait_ge(S["q_lo"], 4 * n + 2)
                    pe.wait_ge(S["b_evac"], s)
                    broadcast(p, 0, psB, S["b_bcast"])
                state_sum(n, p)

            def c_rows(n, p):
                s = SLOTS * n + p
                pe.wait_ge(S["cmult"], s - 2 + CREDIT["cmult"])
                broadcast((p - 3) % SLOTS, NS, psC, S["c_bcast"])

            def state_sum(n, p):
                q = (p - 4) % SLOTS
                t = q // PAIRS
                if q % PAIRS == 0:
                    pe.wait_ge(S["y_evac"], 6 * n + t)
                    if t in (2, 3):
                        pe.wait_ge(S["conv_read"], 2 * n + t - 1)
                for j in range(2):
                    ins = mm(psY[:, t % 2, 0:NP], w("ident"), hC[:, q % 2, NP * j:NP * j + NP],
                             start=q % PAIRS == 0 and j == 0, stop=q % PAIRS == PAIRS - 1 and j == 1)
                ins.then_inc(S["reduced"], 1)

            def center_y(ph, f, n, name, wa, wlo, whi, rows):
                if name == "cenA":
                    pe.wait_ge(S["yas_made"], f + 1)
                    pe.wait_ge(S["y_evac"], 6 * f + 1)
                open_side(ph, name, n)
                ps = side_ps(ph, name, NP, rows)
                mm(ps, wa, yAs, start=True, stop=False)
                mm(ps, wlo, ysM, start=False, stop=False)
                done_side(ph, name, mm(ps, whi, turned(ysM), start=False, stop=True))

            def var_y(ph, n):
                wait_read(pe, ph, "cenA", n)
                wait_read(pe, ph, "cenB", n)
                open_side(ph, "varY", n)
                mm(side_ps(ph, "varY"), w("one192"), sY[:, 0, :], start=True, stop=False)
                done_side(ph, "varY", mm(side_ps(ph, "varY"), w("one192", DB), sY[0:DB, 1, :], start=False, stop=True))

            def out_project(ph, f, n):
                pe.wait_ge(S["gated"], f + 1)
                open_side(ph, "outp", n)
                mm(side_ps(ph, "outp", NP, C), w("owa"), cY[:, 0, :], start=True, stop=False)
                done_side(ph, "outp", mm(side_ps(ph, "outp", NP, C), w("owb", DB), cY[0:DB, 1, :], start=False, stop=True))

            def finish(ph, f, n, name):
                if name == "cenA":
                    center_y(ph, f, n, "cenA", w("cenaa"), w("cenalo"), w("cenahi"), 128)
                if name == "cenB":
                    center_y(ph, f, n, "cenB", w("cenba"), w("cenblo"), w("cenbhi"), DB)
                if name == "varY":
                    var_y(ph, n)
                if name == "outp":
                    out_project(ph, f, n)

            def fill_side(n, m, name):
                if name in F_SIDE:
                    finish(sides, n, n, name)
                elif name[:2] == "xp":
                    project_x(n, int(name[2:]))
                elif name[:2] == "dt":
                    steps(n, int(name[2:]))
                elif name[:2] == "up":
                    up(sides, m, n, int(name[2]), int(name[4]))
                elif name == "center":
                    pe.wait_ge(S["h0_made"], n + 1)
                    one(sides, name, n, w("cen96", C), h0[:, :], C)
                elif name == "var":
                    wait_read(pe, sides, "center", n)
                    one(sides, name, n, w("one96", C), sq[:, :], C)
                elif name != "down":
                    if name == "inA":
                        pe.wait_ge(S["xn_made"], n + 1)
                    in_project(n, ("inA", "inB", "inZA", "inZB").index(name))

            def l0_only(m, r):
                for t in range(MT):
                    up(sides_l0, m, m, t, 0)
                    up(sides_l0, m, m, t, 1)
                for t in DOWN:
                    down(sides_l0, m, m, t)

            def iteration(n, b, r):
                order.clear()
                m = n + NWR
                for p in range(SLOTS):
                    scan_slot(n, p)
                    for name, slot, _ in SIDE:
                        if slot == p:
                            fill_side(n, m, name)
                    for t, slot in DOWN.items():
                        if slot == p:
                            down(sides, m, n, t)
                    if 15 <= p < 18:
                        window_conv(n, 0, p - 15)
                    if 20 <= p < 23:
                        window_conv(n, 1, p - 20)
                assert order == [x for x, _, _ in SIDE]

            def last(f):
                c_rows(f, 0)
                state_sum(f, 0)
                c_rows(f, 1)
                state_sum(f, 1)
                c_rows(f, 2)
                state_sum(f, 2)
                c_rows(f, 3)
                state_sum(f, 3)
                for name in F_SIDE:
                    finish(sides_f, f, 0, name)

            pe.wait_ge(S["packed"], 16)
            for j in range(4):
                ins = mm(psY[:, 0, j:j + 1], w("inw", C, 128 * j, 128), w("lnb", C), start=True, stop=True)
            ins.then_inc(S["inw_done"], 1)
            pe.wait_ge(S["zeroed_a"], 1)
            pe.wait_ge(S["zeroed_b"], 1)
            mm(psY[:, 1, 0:NP], w("ident"), ysA, start=True, stop=False)
            pe.wait_ge(S["folded_ready"], 1)
            over_chunks(pe, l0_only, lambda b: None, iteration, last)

        @block.scalar
        def _(act):
            do = nc.scalar.activation

            def up_read(ph, m, n, t, half):
                name = f"up{t}_{half}"
                act.wait_ge(S["taps"], 9 * len(TAPS) * m)
                wait_side(act, ph, name, n)
                R = rows_of(t)
                do(mid[0:R, t, 5 * half:5 * half + 5, 1:HW + 1],
                   side_ps(ph, name, HH, R).rearrange("p (r c) -> p r c", c=HW), ACT.Relu,
                   bias=o1[0:R, t:t + 1], scale=s1[0:R, t:t + 1]).then_inc(side_read[ph.bank(name)], 1)

            def depthwise_read(m, t):
                R = rows_of(t)
                if t in TAPS:
                    act.wait_ge(S["taps"], 9 * (len(TAPS) * m + TAP_TURN[t] + 1))
                else:
                    act.wait_ge(S["shared_sums"], 8 * (len(SHARED) * m + SHARED_TURN[t] + 1) + CREDIT["shared_sums"])
                do(z2[0:R, t, :], z2[0:R, t, :], ACT.Relu, bias=o2[0:R, t:t + 1],
                   scale=s2[0:R, t:t + 1]).then_inc(S["z2_made"], 1)

            def tap_product(m, t, k):
                R, turn = rows_of(t), len(SHARED) * m + SHARED_TURN[t]
                if k == 0:
                    act.wait_ge(S["mid_masked"], MT * m + t + 1)
                else:
                    act.wait_ge(S["shared_sums"], 8 * turn + k - 2 + CREDIT["shared_sums"])
                dst = z2[0:R, t, :] if k == 0 else product[0:R, k % 2, :]
                do(dst.rearrange("p (r c) -> p r c", c=HW), mid[0:R, t, k // 3:k // 3 + WS, k % 3:k % 3 + HW],
                   ACT.Copy, scale=w("wd", R, 9 * t + k, 1)).then_inc(S["products"], 1)

            def down_read(ph, m, n):
                act.wait_ge(S["x1_made"], m)
                wait_side(act, ph, "down", n)
                do(y3[:, :], side_ps(ph, "down", NP, C), ACT.Identity, bias=o3[0:C, :],
                   scale=s3[0:C, :]).then_inc(side_read[ph.bank("down")], 1)

            def sigmoid_tail(buf, ready, ln_made, made, n):
                act.wait_ge(ready, n + 1)
                do(buf, buf, ACT.Ln).then_inc(ln_made, 1)
                act.wait_ge(ln_made, n + 1)
                do(buf, buf, ACT.Exp, scale=-1.0).then_inc(made, 1)

            def hi_parts(n, k):
                name = f"xp{k}"
                wait_side(act, sides, name, n)
                do(Q[:, k, :], side_ps(sides, name), ACT.Copy)
                do(Fk[:, k % 2, :], side_ps(sides, name, NP, 64), ACT.Copy).then_inc(S["f_made"], 1)

            def mid_part(n, k):
                wait_read(act, sides, f"xp{k}", n)
                do(Q[64:128, k, :], rest[64:128, k % 2, :], ACT.Copy).then_inc(S["q_mid"], 1)

            def step_abs(n, t):
                i, name = DT_TURN[t] % 2, f"dt{t}"
                act.wait_ge(S["delta_made"], 6 * n + DT_TURN[t] - 1 + CREDIT["delta_made"])
                wait_side(act, sides, name, n)
                do(dta_[:, i, :], side_ps(sides, name), ACT.Abs, bias=w("dtb", 128, t, 1)).then_inc(S["abs_made"], 1)
                do(dtm_[:, i, :], side_ps(sides, name), ACT.Relu, bias=w("dtb", 128, t, 1))\
                    .then_inc(side_read[sides.bank(name)], 1)

            def step_exp(n, t):
                i = DT_TURN[t] % 2
                act.wait_ge(S["abs_made"], 6 * n + DT_TURN[t] + 1)
                do(dte[:, i, :], dta_[:, i, :], ACT.Exp, scale=-1.0).then_inc(S["exp_made"], 1)

            def step_log(n, t):
                i = DT_TURN[t] % 2
                act.wait_ge(S["exp_made"], 6 * n + DT_TURN[t] + 1)
                do(dtl[:, i, :], dte[:, i, :], ACT.Ln, bias=1.0).then_inc(S["log_made"], 1)

            def scan_slot(n, p):
                s = SLOTS * n + p
                t, n0 = p // PAIRS, 2 * (p % PAIRS)
                act.wait_ge(S["b_bcast"], s + 1)
                act.wait_ge(S["dbu_made"], s + 1)
                do(Bsb[:, p % 2, :].rearrange("p (j f) -> p j f", j=2), psB[:, :, 0:NP], ACT.Copy)\
                    .then_inc(S["b_evac"], 1)
                if p % PAIRS == 0:
                    act.wait_ge(S["delta_made"], 6 * n + t)
                act.wait_ge(S["scanned"], s + 1)
                back = int(t >= 3)
                keep = slice(0, WP - 1) if back else slice(1, WP)
                src = delta[:, t, :].rearrange("p (w q) -> p w q", q=WP)[:, :, keep]
                for j in range(2):
                    dst = dA[:, p % 2, back + NP * j:back + NP * j + NP].rearrange("p (w q) -> p w q", q=WP)[:, :, keep]
                    ins = do(dst, src, ACT.Exp, scale=A[:, NS * t + n0 + j:NS * t + n0 + j + 1])
                ins.then_inc(S["da_made"], 1)

            def finish(ph, f, n, p):
                if p == AT["cenB"] + 1:
                    for a, (name, R) in enumerate((("cenA", 128), ("cenB", DB))):
                        wait_side(act, ph, name, n)
                        do(cY[0:R, a, :], side_ps(ph, name, NP, R), ACT.Copy)
                        do(sY[0:R, a, :], side_ps(ph, name, NP, R), ACT.Square).then_inc(side_read[ph.bank(name)], 1)
                if p == AT["varY"] + 1:
                    wait_side(act, ph, "varY", n)
                    do(rY, side_ps(ph, "varY"), ACT.Ln, bias=sb_eps[:, 0:1]).then_inc(side_read[ph.bank("varY")], 1)
                    wait_read(act, ph, "varY", n)
                    do(rY, rY, ACT.Exp, scale=-0.5).then_inc(S["ry_made"], 1)
                if p == AT["outp"] + 1:
                    wait_side(act, ph, "outp", n)
                    act.wait_ge(S["out_made"], f)
                    do(outs[:, :], side_ps(ph, "outp", NP, C), ACT.Copy).then_inc(side_read[ph.bank("outp")], 1)

            def l0_only(m, r):
                for t in range(MT):
                    up_read(sides_l0, m, m, t, 0)
                    up_read(sides_l0, m, m, t, 1)
                for t in SHARED:
                    for k in range(9):
                        tap_product(m, t, k)
                for t in DOWN:
                    depthwise_read(m, t)
                down_read(sides_l0, m, m)

            def boundary(b):
                act.wait_ge(S["aggregated"], b + 1)
                do(coef[:, 0:1], meanvar[:, 1:2], ACT.Ln, bias=sb_eps[0:C, 0:1]).then_inc(S["rstd_ln"], 1)
                act.wait_ge(S["rstd_ln"], b + 1)
                do(coef[:, 0:1], coef[:, 0:1], ACT.Exp, scale=-0.5).then_inc(S["rstd_made"], 1)

            def slots(n, b, first, end):
                m = n + NWR
                for p in range(first, end):
                    scan_slot(n, p)
                    if p == 3:
                        hi_parts(n, 2)
                        hi_parts(n, 3)
                    if p == 6:
                        mid_part(n, 2)
                        mid_part(n, 3)
                    if p == 2:
                        act.wait_ge(S["x1_loaded"], 16 * n + 16)
                        act.wait_ge(S["coef_made"], b + 1)
                        do(v[:, :], x1r[:, :], ACT.Identity, bias=coef[:, 3:4], scale=coef[:, 1:2]).then_inc(S["v_made"], 1)
                        act.wait_ge(S["v_made"], n + 1)
                        do(sigh[:, :], v[:, :], ACT.Exp, scale=-1.0).then_inc(S["eh_made"], 1)
                    if p == 4:
                        sigmoid_tail(sigh[:, :], S["e1h_made"], S["lh_made"], S["sgh_made"], n)
                    finish(sides, n, n, p)
                    if p == AT["center"] + 1:
                        wait_side(act, sides, "center", n)
                        do(cen[:, :], side_ps(sides, "center", NP, C), ACT.Copy)
                        do(sq[:, :], side_ps(sides, "center", NP, C), ACT.Square).then_inc(side_read[sides.bank("center")], 1)
                    if p == AT["var"] + 1:
                        wait_side(act, sides, "var", n)
                        do(sq[:, :], side_ps(sides, "var", NP, C), ACT.Ln, bias=sb_eps[0:C, 0:1])\
                            .then_inc(side_read[sides.bank("var")], 1)
                        wait_read(act, sides, "var", n)
                        do(sq[:, :], sq[:, :], ACT.Exp, scale=-0.5).then_inc(S["rs_made"], 1)
                    if p == AT["inA"] + 1:
                        for name, j, parts in (("inA", 0, ((xpA, 0, 128, 1),)),
                                               ("inB", 1, ((xpB, 0, DB, 1), (xpB, DB, 128, 0)))):
                            wait_side(act, sides, name, n)
                            for xp, a, e, left in parts:
                                ins = do(xp[a:e, :, 1:WS + 1, left:left + WS], win(side_ps(sides, name)[a:e]), ACT.Identity,
                                         bias=inbias[a:e, j:j + 1])
                            ins.then_inc(side_read[sides.bank(name)], 1)
                    if p == AT["inZA"] + 1:
                        for name, j in (("inZA", 0), ("inZB", 1)):
                            wait_side(act, sides, name, n)
                            do(vz[:, j, :], side_ps(sides, name), ACT.Identity, bias=inbias[:, 2 + j:3 + j])\
                                .then_inc(side_read[sides.bank(name)], 1)
                    if p == 23:
                        wait_read(act, sides, "inZA", n)
                        wait_read(act, sides, "inZB", n)
                        do(sigz[:, :, :], vz[:, :, :], ACT.Exp, scale=-1.0).then_inc(S["ez_made"], 1)
                    for q, j, cb in ((18, 0, "cba"), (23, 1, "cbb")):
                        if p == q:
                            act.wait_ge(S["conv_made"], 2 * n + 1 + j)
                            do(vu[:, j, :], psY[:, j, 0:NP], ACT.Identity, bias=w(cb)).then_inc(S["conv_read"], 1)
                    if p == 26:
                        sigmoid_tail(sigz[:, :, :], S["e1z_made"], S["lz_made"], S["sgz_made"], n)
                    if p == 24:
                        act.wait_ge(S["conv_read"], 2 * n + 2)
                        do(sigu[:, :, :], vu[:, :, :], ACT.Exp, scale=-1.0).then_inc(S["eu_made"], 1)
                    if p == 27:
                        sigmoid_tail(sigu[:, :, :], S["e1u_made"], S["lu_made"], S["sgu_made"], n)
                    if p == 30:
                        act.wait_ge(S["u_made"], n + 1)
                        do(turned(uM[DB:128]), win(vu[DB:128, 1, :]), ACT.Copy).then_inc(S["um_made"], 1)
                    if p == 32:
                        hi_parts(n, 0)
                        hi_parts(n, 1)
                    if p == 35:
                        mid_part(n, 0)
                        mid_part(n, 1)
                    for t, q in DT_SLOT.items():
                        if p == q + 1:
                            step_abs(n, t)
                        if p == q + 2:
                            step_exp(n, t)
                        if p == q + 3:
                            step_log(n, t)
                    for t in range(MT):
                        for half in range(2):
                            if p == AT[f"up{t}_{half}"] + 1:
                                up_read(sides, m, n, t, half)
                        if p == (TAPS | SHARED)[t][1] + 1:
                            depthwise_read(m, t)
                    for t, k in taps_in(SHARED, p):
                        tap_product(m, t, k)
                    if p == 47:
                        down_read(sides, m, n)

            def iteration(n, b, r):
                slots(n, b, ACT_HEAD, SLOTS)
                slots(n + 1, b, 0, ACT_HEAD)

            def last(f):
                for name in ("cenB", "varY", "outp"):
                    finish(sides_f, f, 0, AT[name] + 1)

            nc.scalar.preload_act_table_set("natural_log_exp_and_others")
            act.wait_ge(S["packed"], 16)
            act.wait_ge(S["zeroed_a"], 1)
            act.wait_ge(S["zeroed_b"], 1)
            for i, (dst, src, R) in enumerate(((s1, "v1", 128), (s2, "v2", 128), (s3, "v3", C))):
                do(dst[0:R, :], w(src, R), ACT.Ln, bias=sb_eps[0:R, 0:1]).then_inc(S["bn_ln"], 1)
                act.wait_ge(S["bn_ln"], i + 1)
                do(dst[0:R, :], dst[0:R, :], ACT.Exp, scale=-0.5).then_inc(S["bn_rs"], 1)
            do(A[:, :], w("alog"), ACT.Exp).then_inc(S["bn_rs"], 1)
            act.wait_ge(S["inw_done"], 1)
            do(inbias[:, :], psY[:, 0, 0:4], ACT.Copy).then_inc(S["inb"], 1)
            act.wait_ge(S["inb"], 1)
            act.wait_ge(S["folded_ready"], 1)
            over_chunks(act, l0_only, boundary, iteration, last, slots)

        @block.vector
        def _(dve):
            V = nc.vector

            def tap(m, t, k):
                R = rows_of(t)
                done = 9 * (len(TAPS) * m + TAP_TURN[t]) + k
                src = mid[0:R, t, k // 3:k // 3 + WS, k % 3:k % 3 + HW]
                dst = z2[0:R, t, :].rearrange("p (r c) -> p r c", c=HW)
                wk = w("wd", R, 9 * t + k, 1)
                if k == 0:
                    dve.wait_ge(S["mid_masked"], MT * m + t + 1)
                    V.tensor_scalar(dst, src, wk, None, ALU.mult).then_inc(S["taps"], 1)
                else:
                    dve.wait_ge(S["taps"], done)
                    V.scalar_tensor_tensor(out=dst, in0=src, scalar=wk, in1=dst, op0=ALU.mult, op1=ALU.add)\
                        .then_inc(S["taps"], 1)

            def stat(m, r):
                dve.wait_ge(S["x1_made"], m + 1)
                V.bn_stats(stats[:, bass.ds(r * 6, 6)], x1o[:, :]).then_inc(S["stats_made"], 1)

            def cap_and_one(buf, ready, made, n):
                dve.wait_ge(ready, n + 1)
                V.tensor_scalar(buf, buf, EXP_CAP, 1.0, ALU.min, ALU.add).then_inc(made, 1)

            def rests(n, k):
                name = f"xp{k}"
                dve.wait_ge(S["f_made"], 4 * n + (k + 2) % 4 + 1)
                V.tensor_tensor(rest[64:128, k % 2, :], side[64:128, sides.bank(name), 0:NP], Q[64:128, k, :],
                                ALU.subtract).then_inc(side_read[sides.bank(name)], 1)

            def lo_part(n, k):
                dve.wait_ge(S["q_mid"], 4 * n + (k + 2) % 4 + 1)
                V.tensor_tensor(Q[96:128, k, :], rest[96:128, k % 2, :], Q[96:128, k, :], ALU.subtract)\
                    .then_inc(S["q_lo"], 1)

            def log_select(n, t):
                i, turn = DT_TURN[t] % 2, 6 * n + DT_TURN[t]
                dve.wait_ge(S["log_made"], turn + 1)
                V.scalar_tensor_tensor(out=dtl[:, i, :], in0=dte[:, i, :], scalar=LN_SMALL, in1=dtl[:, i, :],
                                       op0=ALU.is_ge, op1=ALU.mult).then_inc(S["logsel_made"], 1)

            def log_max(n, t):
                i, turn = DT_TURN[t] % 2, 6 * n + DT_TURN[t]
                dve.wait_ge(S["logsel_made"], turn + 1)
                dve.wait_ge(S["poly_made"], turn + 1)
                V.tensor_tensor(dtl[:, i, :], dtl[:, i, :], dtp[:, i, :], ALU.max).then_inc(S["logmax_made"], 1)

            def step_size(n, t):
                i, turn = DT_TURN[t] % 2, 6 * n + DT_TURN[t]
                dve.wait_ge(S["logmax_made"], turn + 1)
                V.tensor_tensor(delta[:, t, :], dtl[:, i, :], dtm_[:, i, :], ALU.add).then_inc(S["delta_made"], 1)

            def scan_slot(n, p):
                s = SLOTS * n + p
                back = int(p // PAIRS >= 3)
                dve.wait_ge(S["da_made"], s + 1)
                dve.wait_ge(S["dbu_made"], s + 1 + CREDIT["dbu_made"])
                dve.wait_ge(S["cmult"], s - 1 + CREDIT["cmult"])
                step = -1 if back else 1
                V.tensor_tensor_scan(h[:, p % 3, ::step], dA[:, p % 2, back:back + 2 * NP][:, ::step], dBu[:, p % 2, ::step],
                                     0.0, ALU.mult, ALU.add).then_inc(S["scanned"], 1)
                times_c(n, p)

            def times_c(n, p):
                s = SLOTS * n + p
                q = (p - 1) % SLOTS
                dve.wait_ge(S["c_bcast"], s + 3)
                dve.wait_ge(S["scanned"], s + CREDIT["scanned"])
                dve.wait_ge(S["reduced"], s + 2)
                V.tensor_tensor(hC[:, q % 2, :].rearrange("p (j f) -> p j f", j=2),
                                h[:, q % 3, :].rearrange("p (j f) -> p j f", j=2), psC[:, :, 0:NP],
                                ALU.mult).then_inc(S["cmult"], 1)

            def take_y(n, t, turn):
                p = (PAIRS * t + PAIRS + 3) % SLOTS
                dve.wait_ge(S["reduced"], SLOTS * n + p + 1)
                y = psY[:, t % 2, 0:NP]
                if t == 0:
                    ins = V.scalar_tensor_tensor(out=ysA, in0=uA, scalar=Dm[:, 0:1], in1=y, op0=ALU.mult, op1=ALU.add)
                elif t == 1:
                    ins = V.tensor_copy(ysAT, y)
                elif t == 2:
                    ins = V.scalar_tensor_tensor(out=ysM, in0=uM, scalar=Dm[:, 1:2], in1=y, op0=ALU.mult, op1=ALU.add)
                else:
                    ys = (ysA, ysAT, ysM)[t - 3]
                    ins = V.tensor_tensor(ys, ys, y, ALU.add)
                ins.then_inc(S["y_evac"], 1)

            def finish(f, p):
                parts = ((0, 128, "oga", "oba"), (1, DB, "ogb", "obb"))
                if p == AT["varY"] + 2:
                    dve.wait_ge(S["ry_made"], f + 1)
                    for a, R, g, _ in parts:
                        ins = V.scalar_tensor_tensor(out=cY[0:R, a, :], in0=cY[0:R, a, :], scalar=w(g, R),
                                                     in1=rY[0:R, :], op0=ALU.mult, op1=ALU.mult)
                    ins.then_inc(S["norm_made"], 1)
                if p == AT["varY"] + 3:
                    dve.wait_ge(S["norm_made"], f + 1)
                    dve.wait_ge(S["rotated"], 32 * f)
                    for a, R, _, o in parts:
                        ins = V.scalar_tensor_tensor(out=cY[0:R, a, :], in0=cY[0:R, a, :], scalar=w(o, R),
                                                     in1=gateF[0:R, a, :], op0=ALU.add, op1=ALU.mult)
                    ins.then_inc(S["gated"], 1)

            def l0_only(m, r):
                for t in TAPS:
                    for k in range(9):
                        tap(m, t, k)
                stat(m, r)

            def boundary(b):
                wait_apart(dve, S["stats_made"], NWR * (b + 1))
                V.bn_aggr(meanvar[:, :], stats[:, :].rearrange("p (r s) -> p r s", s=6)).then_inc(S["aggregated"], 1)
                dve.wait_ge(S["rstd_made"], b + 1)
                V.tensor_tensor(coef[:, 1:2], coef[:, 0:1], w("gamma", C), ALU.mult).then_inc(S["scale_made"], 1)
                dve.wait_ge(S["scale_made"], 2 * b + 1)
                V.tensor_tensor(coef[:, 2:3], coef[:, 1:2], meanvar[:, 0:1], ALU.mult).then_inc(S["scale_made"], 1)
                dve.wait_ge(S["scale_made"], 2 * b + 2)
                V.tensor_tensor(coef[:, 3:4], w("beta", C), coef[:, 2:3], ALU.subtract).then_inc(S["coef_made"], 1)

            def iteration(n, b, r):
                m = n + NWR
                for p in range(SLOTS):
                    mine = taps_in(TAPS, p)
                    if len(mine) == 2:
                        tap(m, *mine[0])
                    if p == 4:
                        rests(n, 2)
                        rests(n, 3)
                    if p == 33:
                        rests(n, 0)
                        rests(n, 1)
                    for t, q in DT_SLOT.items():
                        if p == q + 4:
                            log_select(n, t)
                        if p == q + 5:
                            step_size(n, t)
                    scan_slot(n, p)
                    if p == 2:
                        take_y(n, 5, 0)
                    if p % PAIRS == 2 and p > 2:
                        take_y(n, p // PAIRS - 1, p // PAIRS)
                    if p == 7:
                        lo_part(n, 2)
                        lo_part(n, 3)
                    if p == 2:
                        cap_and_one(sigh[:, :], S["eh_made"], S["e1h_made"], n)
                    finish(n, p)
                    if p == 24:
                        cap_and_one(sigz[:, :, :], S["ez_made"], S["e1z_made"], n)
                    if p == 25:
                        cap_and_one(sigu[:, :, :], S["eu_made"], S["e1u_made"], n)
                    if p == 28:
                        dve.wait_ge(S["sgu_made"], n + 1)
                        dve.wait_ge(S["dtu_made"], 6 * n + 3 + CREDIT["dtu_made"])
                        dve.wait_ge(S["y_evac"], 6 * n + 4)
                        V.tensor_tensor(uA, vu[:, 0, :], sigu[:, 0, :], ALU.mult)
                        V.tensor_tensor(uM[0:DB], vu[0:DB, 1, :], sigu[0:DB, 1, :], ALU.mult)
                        V.tensor_tensor(vu[DB:128, 1, :], vu[DB:128, 1, :], sigu[DB:128, 1, :], ALU.mult)\
                            .then_inc(S["u_made"], 1)
                    if p == 36:
                        lo_part(n, 0)
                        lo_part(n, 1)
                    for t, q in DT_SLOT.items():
                        if p == q + 4:
                            log_max(n, t)
                    if mine:
                        tap(m, *mine[-1])
                    if p == 47:
                        stat(m, r)

            def last(f):
                times_c(f, 0)
                take_y(f, 5, 0)
                finish(f, AT["varY"] + 2)
                finish(f, AT["varY"] + 3)

            V.memset(Z[:, 0:len_a], 0.0).then_inc(S["zeroed_a"], 1)
            dve.wait_ge(S["packed"], 16)
            dve.wait_ge(S["zeroed_b"], 1)
            dve.sem_inc(S["scanned"], CREDIT["scanned"])
            dve.sem_inc(S["cmult"], CREDIT["cmult"])
            dve.sem_inc(S["delta_made"], CREDIT["delta_made"])
            V.tensor_copy(sel[:, :, :], w("selcol").unsqueeze(2).to_broadcast([128, 32, 128]))
            for tapk in range(9):
                V.tensor_scalar(diagA[:, tapk, :], w("ident"), w("cwa", 128, tapk, 1), None, ALU.mult)
            for pair in range(6):
                V.tensor_scalar(diagB[:, pair, :], w("twice"), w("cwb", 128, pair, 1), None, ALU.mult)
            V.reduce_sum(Dm[:, 0:1], w("dsa"), axis=mybir.AxisListType.X)
            V.reduce_sum(Dm[:, 1:2], w("dsm"), axis=mybir.AxisListType.X)
            dve.wait_ge(S["bn_rs"], 4)
            V.tensor_scalar(A[:, :], A[:, :], -1.0, None, ALU.mult)
            bns = ((s1, o1, "1", 128), (s2, o2, "2", 128), (s3, o3, "3", C))
            for s_, o_, i, R in bns:
                ins = V.tensor_tensor(s_[0:R, :], s_[0:R, :], w("g" + i, R), ALU.mult)
            ins.then_inc(S["folded_bn"], 1)
            dve.wait_ge(S["folded_bn"], 1)
            for s_, o_, i, R in bns:
                ins = V.tensor_tensor(o_[0:R, :], s_[0:R, :], w("m" + i, R), ALU.mult)
            ins.then_inc(S["folded_bn"], 1)
            dve.wait_ge(S["folded_bn"], 2)
            for s_, o_, i, R in bns:
                ins = V.tensor_tensor(o_[0:R, :], w("b" + i, R), o_[0:R, :], ALU.subtract)
            dve.wait_ge(S["inw_done"], 1)
            V.tensor_scalar(w("inw", C), w("inw", C), w("lng", C), None, ALU.mult)
            V.tensor_scalar(w("owa"), w("owa"), w("alpha"), None, ALU.mult)
            V.tensor_scalar(w("owb", DB), w("owb", DB), w("alpha", DB), None, ALU.mult).then_inc(S["folded_ready"], 1)
            dve.wait_ge(S["folded_ready"], 1)
            over_chunks(dve, l0_only, boundary, iteration, last)

        @block.gpsimd
        def _(pool):
            G = nc.gpsimd

            def mask_rows(ph, m, n, r, t):
                for half in range(2):
                    name = f"up{t}_{half}"
                    wait_apart(pool, side_read[ph.bank(name)], ph.fills(name, n))
                R = rows_of(t)
                for side_, row in ((0, 0), (1, XP - 1)):
                    edge = mid[0:R, t, row, 1:HW + 1]
                    ins = G.tensor_tensor(edge, edge, masks[0:R, bass.ds((r * 2 + side_) * HW, HW)], ALU.mult)
                ins.then_inc(S["mid_masked"], 1)

            def tap_sum(m, t, k):
                R, turn = rows_of(t), len(SHARED) * m + SHARED_TURN[t]
                pool.wait_ge(S["products"], 9 * turn + k + 1)
                pool.wait_ge(S["shared_sums"], 8 * turn + k - 1 + CREDIT["shared_sums"])
                G.tensor_tensor(z2[0:R, t, :], z2[0:R, t, :], product[0:R, k % 2, :], ALU.add)\
                    .then_inc(S["shared_sums"], 1)

            def residual_l0(ph, m, n):
                wait_read(pool, ph, "down", n)
                pool.wait_ge(S["x1_stored"], 16 * m)
                pool.wait_ge(S["stats_made"], m)
                pool.wait_ge(S["x_loaded"], 16 * m + 16)
                G.tensor_tensor(win(x1o[:, :]), image_rows(y3[:, :]), image_rows(xin[:, HW:HW + NP]), ALU.add)\
                    .then_inc(S["x1_made"], 1)

            def poly(n, t):
                i, turn = DT_TURN[t] % 2, 6 * n + DT_TURN[t] + 1
                wait_apart(pool, S["exp_made"], turn)
                G.tensor_scalar(dtp[:, i, :], dte[:, i, :], -0.5, 1.0, ALU.mult, ALU.add).then_inc(S["poly0_made"], 1)
                pool.wait_ge(S["poly0_made"], turn)
                G.tensor_tensor(dtp[:, i, :], dtp[:, i, :], dte[:, i, :], ALU.mult).then_inc(S["poly_made"], 1)

            def step_u(n, t):
                pool.wait_ge(S["delta_made"], 6 * n + DT_TURN[t] + 1 + CREDIT["delta_made"])
                G.tensor_tensor(dtu[:, t, :], delta[:, t, :], (uA, uAT, uM)[t % 3], ALU.mult).then_inc(S["dtu_made"], 1)

            def scan_slot(n, p):
                s = SLOTS * n + p
                t = p // PAIRS
                if p % PAIRS == 0:
                    pool.wait_ge(S["dtu_made"], 6 * n + t)
                pool.wait_ge(S["b_evac"], s + 1)
                pool.wait_ge(S["scanned"], s + 1)
                G.tensor_tensor(dBu[:, p % 2, :].rearrange("p (j f) -> p j f", j=2),
                                Bsb[:, p % 2, :].rearrange("p (j f) -> p j f", j=2),
                                dtu[:, t, :].unsqueeze(1).to_broadcast([128, 2, NP]), ALU.mult).then_inc(S["dbu_made"], 1)

            def finish(ph, f, n, p):
                if p == 4:
                    pool.wait_ge(S["y_evac"], 6 * f + 1)
                    G.tensor_tensor(win(yAs), win(ysA), turned(ysAT), ALU.add).then_inc(S["yas_made"], 1)
                if p == AT["outp"] + 2:
                    wait_read(pool, ph, "outp", n)
                    pool.wait_ge(S["rotated"], 32 * f)
                    pool.wait_ge(S["out_stored"], 16 * f)
                    G.tensor_tensor(outb[:, :], outs[:, :], residF[0:C, :], ALU.add).then_inc(S["out_made"], 1)

            def l0_only(m, r):
                for t in range(MT):
                    mask_rows(sides_l0, m, m, r, t)
                for t in SHARED:
                    for k in range(1, 9):
                        tap_sum(m, t, k)
                residual_l0(sides_l0, m, m)

            def iteration(n, b, r):
                m = n + NWR
                for p in range(SLOTS):
                    scan_slot(n, p)
                    finish(sides, n, n, p)
                    if p == 5:
                        pool.wait_ge(S["sgh_made"], n + 1)
                        G.tensor_tensor(h0[:, :], v[:, :], sigh[:, :], ALU.mult).then_inc(S["h0_made"], 1)
                    if p == 11:
                        pool.wait_ge(S["rs_made"], n + 1)
                        G.tensor_tensor(sq[:, :], cen[:, :], sq[:, :], ALU.mult).then_inc(S["xn_made"], 1)
                    if p == 28:
                        pool.wait_ge(S["sgz_made"], n + 1)
                        G.tensor_tensor(gateP[:, :, :], vz[:, :, :], sigz[:, :, :], ALU.mult).then_inc(S["gate_made"], 1)
                    if p == 23:
                        wait_apart(pool, S["h0_made"], n + 1)
                        G.tensor_scalar(v[:, :], h0[:, :], w("alpha", C), 0.0, ALU.mult, ALU.add).then_inc(S["alphah_made"], 1)
                        pool.wait_ge(S["rotated"], 32 * n + 32)
                        pool.wait_ge(S["alphah_made"], n + 1)
                        G.tensor_tensor(residP[0:C, :], v[:, :], x1r[:, :], ALU.add).then_inc(S["resid_made"], 1)
                    if p == 28:
                        pool.wait_ge(S["y_evac"], 6 * n + 4)
                        pool.wait_ge(S["sgu_made"], n + 1)
                        G.tensor_tensor(turned(uAT), win(vu[:, 0, :]), win(sigu[:, 0, :]), ALU.mult).then_inc(S["ut_made"], 1)
                    for t, q in DT_SLOT.items():
                        if p == q + 3:
                            poly(n, t)
                        if p == q + 7:
                            step_u(n, t)
                    for t in range(MT):
                        if p == AT[f"up{t}_1"] + 2:
                            mask_rows(sides, m, n, r, t)
                    for t, k in taps_in(SHARED, p - 1):
                        if k > 0:
                            tap_sum(m, t, k)
                    if p == 47:
                        residual_l0(sides, m, n)

            def last(f):
                finish(sides_f, f, 0, 4)
                finish(sides_f, f, 0, AT["outp"] + 2)

            G.memset(Z[:, len_a:], 0.0)
            G.memset(sb_eps[:, :], EPS).then_inc(S["zeroed_b"], 1)
            pool.sem_inc(S["dbu_made"], CREDIT["dbu_made"])
            pool.sem_inc(S["dtu_made"], CREDIT["dtu_made"])
            pool.sem_inc(S["shared_sums"], CREDIT["shared_sums"])
            pool.wait_ge(S["zeroed_a"], 1)
            pool.wait_ge(S["masks_in"], 16)
            pool.wait_ge(S["folded_ready"], 1)
            over_chunks(pool, l0_only, lambda b: None, iteration, last)


def kernel(**inputs):
    import concourse.bacc as bacc
    from concourse.bass_utils import run_bass_kernel_spmd

    f = {k: np.asarray(a, dtype=a.dtype) for k, a in inputs.items()}
    x = f["x"]
    xp = np.pad(x, ((0, 0), (0, 0), (1, 1), (0, 0)))
    x_dev = np.zeros((CHUNKS + 1 + NWR, C, HALO), x.dtype)
    for r in range(NWR):
        x_dev[r:CHUNKS:NWR] = xp[:, :, WS * r:WS * r + WS + 2, :].reshape(B, C, HALO)

    cols = {}

    def put(name, a):
        a = a.reshape(a.shape[0], -1)
        full = np.zeros((128, COL[name][1]), np.float32)
        full[:a.shape[0], :a.shape[1]] = a
        cols[name] = full

    def by_tile(a):
        a = a.reshape(E6, -1)
        a = np.concatenate([a, np.zeros((MT * 128 - E6, a.shape[1]), a.dtype)])
        return a.reshape(MT, 128, -1).transpose(1, 0, 2).reshape(128, -1)

    put("w1", f["L0_conv_w1"].reshape(E6, C).T)
    put("w3", by_tile(f["L0_conv_w3"].reshape(C, E6).T))
    put("wd", by_tile(f["L0_conv_wd"].reshape(E6, 9)))
    for i in "12":
        for a in "gbm":
            put(a + i, by_tile(f[f"L0_conv_{a}{i}"]))
        var = by_tile(f["L0_conv_v" + i])
        var[E6 - 128 * (MT - 1):, MT - 1] = 1.0
        put("v" + i, var)
    for a in "gbmv":
        put(a + "3", f[f"L0_conv_{a}3"])
    L1 = {k[8:]: a for k, a in f.items() if k.startswith("L1_conv_")}
    put("gamma", L1["gamma"])
    put("beta", L1["beta"])
    put("alpha", np.broadcast_to(L1["alpha"], (128, 1)))
    put("lng", L1["ln1_g"])
    put("lnb", L1["ln1_b"])
    iw = L1["in_proj_w"]
    hi, zhi = iw[:, 128:DN], iw[:, DN + 128:]
    put("inw", np.concatenate([iw[:, :128], hi, hi, iw[:, DN:DN + 128], zhi, zhi], 1))
    cw, cb = L1["conv_w"].reshape(DN, 9), L1["conv_b"]
    put("cwa", cw[:128])
    left, mid_, right_ = (cw[128:, dj::3] for dj in range(3))
    put("cwb", np.concatenate([np.stack([left, right_], 2), np.stack([mid_, np.zeros_like(right_)], 2)]))
    put("cba", cb[:128])
    put("cbb", np.concatenate([cb[128:], cb[128:]]))
    xw = L1["x_proj_w"]
    rows = np.zeros((K, 128, DN), np.float32)
    for at in (0, 64, 96):
        rows[:, at:at + 2 * NS] = xw[:, DTR:]
    rows[:, 32:32 + DTR] = xw[:, :DTR]
    put("xpa", rows[:, :, :128].transpose(2, 0, 1))
    put("xpb", np.concatenate([rows[0::2, :, 128:], rows[1::2, :, 128:]], 2).transpose(2, 0, 1))
    dw = np.zeros((64, K, DN), np.float32)
    dw[32:32 + DTR] = L1["dt_w"].transpose(2, 0, 1)
    put("dta", dw[:, :, :128])
    put("dtm", dw[:, :, 128:])

    def by_scan_tile(a):
        a = a.reshape(K, DN, -1)
        mixed = [np.concatenate([a[k, 128:], a[k + 1, 128:]]) for k in (0, 2)]
        return np.stack([a[0, :128], a[1, :128], mixed[0], a[2, :128], a[3, :128], mixed[1]], 1)

    put("dtb", by_scan_tile(L1["dt_b"]))
    put("alog", by_scan_tile(L1["A_logs"]))
    ds = L1["Ds"].reshape(K, DN).T
    put("dsa", ds[:128])
    put("dsm", ds[128:])
    put("oga", L1["outnorm_g"][:128])
    put("ogb", L1["outnorm_g"][128:])
    put("oba", L1["outnorm_b"][:128])
    put("obb", L1["outnorm_b"][128:])
    put("owa", L1["out_proj_w"][:128])
    put("owb", L1["out_proj_w"][128:])
    put("cen96", np.eye(C, dtype=np.float32) - np.float32(1 / C))
    put("one96", np.full((C, C), 1 / C, np.float32))
    cen = (np.eye(DN, dtype=np.float32) - np.float32(1 / DN))
    zero = np.zeros((DB, 128), np.float32)
    put("cenaa", cen[:128, :128])
    put("cenalo", np.concatenate([cen[128:, :128], zero]))
    put("cenahi", np.concatenate([zero, cen[128:, :128]]))
    put("cenba", cen[:128, 128:])
    put("cenblo", np.concatenate([cen[128:, 128:], zero[:, :DB]]))
    put("cenbhi", np.concatenate([zero[:, :DB], cen[128:, 128:]]))
    put("one192", np.full((128, 128), 1 / DN, np.float32))
    put("ident", np.eye(128, dtype=np.float32))
    put("twice", np.tile(np.eye(DB, dtype=np.float32), (2, 2)))
    e32 = np.eye(32, dtype=np.float32)
    put("selcol", np.concatenate([e32, 0 * e32, e32, e32]))
    pack = np.concatenate([cols[name] for name, _ in PACK], 1)
    m = np.ones((NWR, 2, HW), np.float32)
    m[0, 0] = 0
    m[NWR - 1, 1] = 0
    mask = np.broadcast_to(m.reshape(1, -1), (128, NWR * 2 * HW)).copy()

    nc = bacc.Bacc("TRN2", target_bir_lowering=False, num_devices=1)
    fp32 = mybir.dt.float32
    ins = {"x_dev": x_dev, "pack": pack, "mask": mask}
    aps = {k: nc.dram_tensor(k, a.shape, fp32, kind="ExternalInput").ap() for k, a in ins.items()}
    x1_dram = nc.dram_tensor("x1_dram", (CHUNKS + 1 + NWR, C, NP), fp32).ap()
    out = nc.dram_tensor("out", (CHUNKS + 2, C, NP), fp32, kind="ExternalOutput").ap()
    build(nc, aps["x_dev"], aps["pack"], aps["mask"], x1_dram, out)
    got = run_bass_kernel_spmd(nc, [ins], core_ids=[0]).results[0]["out"]
    y = got[2:].reshape(B, NWR, C, NWR, WS, WS).transpose(0, 2, 1, 4, 3, 5)
    return np.ascontiguousarray(y.reshape(B, C, HW, HW))
```
